# Optimizing a Trainium2 kernel written in Bass

```python
import numpy as np
import jax
import jax.numpy as jnp

def _softmax(x, axis=-1):
    return jax.nn.softmax(x, axis=axis)

def _gelu(x):
    return jax.nn.gelu(x, approximate=True)

def _silu(x):
    return jax.nn.silu(x)

def _sigmoid(x):
    return jax.nn.sigmoid(x)

def _layernorm(x, axis=-1, eps=1e-05):
    m = jnp.mean(x, axis=axis, keepdims=True)
    v = jnp.var(x, axis=axis, keepdims=True)
    return (x - m) / jnp.sqrt(v + eps)

def _scatter_add(tgt, idx, src, axis=0):
    return tgt.at[idx].add(src)

def _segment_sum(src, seg, n):
    return jax.ops.segment_sum(src, seg, n)
kernel_name = 'mk_gnn_resnorm_d1_gnn_r32_399ebe'

def setup_inputs(seed: int=0):
    np.random.seed(seed)
    _w = jnp.asarray

    def _rec_inputs():
        import jax
        import jax.numpy as jnp
        _gk = jax.random.key(seed)
        x = -1.686e-05 + 1 * jax.random.normal(jax.random.fold_in(_gk, 1), (50000, 160), jnp.float32)
        src = jax.random.randint(jax.random.fold_in(_gk, 2), (50000,), 0, 50000, jnp.int32)
        dst = jnp.minimum((50000 * jax.random.uniform(jax.random.fold_in(_gk, 3), (50000,)) ** 2.0).astype(jnp.int32), 49999)
        _o = jnp.argsort(dst, stable=True)
        src = src[_o]
        dst = dst[_o]
        edge_attr_32 = 0.000196303 + 1.00016 * jax.random.normal(jax.random.fold_in(_gk, 11), (50000, 32), jnp.float32)
        node_vec1 = -0.00915711 + 0.999674 * jax.random.normal(jax.random.fold_in(_gk, 13), (50000, 1), jnp.float32)
        return (x, src, dst, edge_attr_32, node_vec1)
    x, src, dst, edge_attr_32, node_vec1 = _rec_inputs()

    def _L0_gnn_setup():
        import jax, jax.numpy as jnp
        import numpy as np
        MUL0_N, MUL1_N = (64, 32)
        MUL0_E, MUL1_E = (8, 8)
        MUL0_H, MUL1_H = (64, 32)
        N_NODES, N_EDGES = (50000, 25000)
        D_NODE = MUL0_N + 3 * MUL1_N
        D_EDGE = MUL0_E + 3 * MUL1_E
        D_HID = MUL0_H + 3 * MUL1_H

        def _split(x, mul0, mul1):
            s = x[..., :mul0]
            v = x[..., mul0:].reshape(x.shape[0], mul1, 3)
            return (s, v)

        def fctp_messages(x, e, W1, W2, W3, W4):
            xs, xv = _split(x, MUL0_N, MUL1_N)
            es, ev = _split(e, MUL0_E, MUL1_E)
            inv_sqrt2 = 1.0 / np.sqrt(2.0)
            s1 = jnp.einsum('ea,eb,abc->ec', xs, es, W1) * (1.0 / np.sqrt(MUL0_N * MUL0_E))
            s2 = jnp.einsum('eai,ebi,abc->ec', xv, ev, W2) * (1.0 / (np.sqrt(3.0) * np.sqrt(MUL1_N * MUL1_E)))
            out_s = (s1 + s2) * inv_sqrt2
            v1 = jnp.einsum('ea,ebi,abc->eci', xs, ev, W3) * (1.0 / np.sqrt(MUL0_N * MUL1_E))
            v2 = jnp.einsum('eai,eb,abc->eci', xv, es, W4) * (1.0 / np.sqrt(MUL1_N * MUL0_E))
            out_v = (v1 + v2) * inv_sqrt2
            return jnp.concatenate([out_s, out_v.reshape(out_v.shape[0], -1)], axis=-1)
        key = jax.random.key(seed)
        ks = jax.random.split(key, 12)
        node_features = jax.random.normal(ks[0], (N_NODES, D_NODE), dtype=jnp.float32)
        edge_index = jax.random.randint(ks[1], (2, N_EDGES), 0, N_NODES, dtype=jnp.int64)
        edge_attr_tensor = jax.random.normal(ks[2], (N_EDGES, D_EDGE), dtype=jnp.float32)
        node_attr_scalar_raw = jax.random.normal(ks[3], (N_NODES, 1), dtype=jnp.float32)
        W1 = jax.random.normal(ks[4], (MUL0_N, MUL0_E, MUL0_H), dtype=jnp.float32)
        W2 = jax.random.normal(ks[5], (MUL1_N, MUL1_E, MUL0_H), dtype=jnp.float32)
        W3 = jax.random.normal(ks[6], (MUL0_N, MUL1_E, MUL1_H), dtype=jnp.float32)
        W4 = jax.random.normal(ks[7], (MUL1_N, MUL0_E, MUL1_H), dtype=jnp.float32)
        Wm = jax.random.normal(ks[8], (D_HID, D_HID), dtype=jnp.float32) / np.sqrt(D_HID)
        bm = jnp.zeros((D_HID,), dtype=jnp.float32)
        Wu = jax.random.normal(ks[9], (D_NODE + D_HID, D_NODE), dtype=jnp.float32) / np.sqrt(D_NODE + D_HID)
        bu = jnp.zeros((D_NODE,), dtype=jnp.float32)
        return {'node_features': node_features, 'edge_index': edge_index, 'edge_attr_tensor': edge_attr_tensor, 'node_attr_scalar_raw': node_attr_scalar_raw, 'W1': W1, 'W2': W2, 'W3': W3, 'W4': W4, 'Wm': Wm, 'bm': bm, 'Wu': Wu, 'bu': bu}
    _L0_gnn_all = _L0_gnn_setup()
    _L0_gnn_in = {k: v for k, v in _L0_gnn_all.items() if k in ('W1', 'W2', 'W3', 'W4', 'Wm', 'bm', 'Wu', 'bu')}
    del _L0_gnn_all
    return {'x': x, 'src': src, 'dst': dst, 'edge_attr_32': edge_attr_32, 'node_vec1': node_vec1, 'L0_gnn_W1': _L0_gnn_in['W1'], 'L0_gnn_W2': _L0_gnn_in['W2'], 'L0_gnn_W3': _L0_gnn_in['W3'], 'L0_gnn_W4': _L0_gnn_in['W4'], 'L0_gnn_Wm': _L0_gnn_in['Wm'], 'L0_gnn_bm': _L0_gnn_in['bm'], 'L0_gnn_Wu': _L0_gnn_in['Wu'], 'L0_gnn_bu': _L0_gnn_in['bu']}

def reference(x, src, dst, edge_attr_32, node_vec1, L0_gnn_W1, L0_gnn_W2, L0_gnn_W3, L0_gnn_W4, L0_gnn_Wm, L0_gnn_bm, L0_gnn_Wu, L0_gnn_bu):
    import jax
    import jax.numpy as jnp

    def _L0_gnn_ref(node_features, edge_index, edge_attr_tensor, node_attr_scalar_raw, W1, W2, W3, W4, Wm, bm, Wu, bu):
        import jax, jax.numpy as jnp
        import numpy as np
        MUL0_N, MUL1_N = (64, 32)
        MUL0_E, MUL1_E = (8, 8)
        MUL0_H, MUL1_H = (64, 32)
        N_NODES, N_EDGES = (50000, 25000)
        D_NODE = MUL0_N + 3 * MUL1_N
        D_EDGE = MUL0_E + 3 * MUL1_E
        D_HID = MUL0_H + 3 * MUL1_H

        def _split(x, mul0, mul1):
            s = x[..., :mul0]
            v = x[..., mul0:].reshape(x.shape[0], mul1, 3)
            return (s, v)

        def fctp_messages(x, e, W1, W2, W3, W4):
            xs, xv = _split(x, MUL0_N, MUL1_N)
            es, ev = _split(e, MUL0_E, MUL1_E)
            inv_sqrt2 = 1.0 / np.sqrt(2.0)
            s1 = jnp.einsum('ea,eb,abc->ec', xs, es, W1) * (1.0 / np.sqrt(MUL0_N * MUL0_E))
            s2 = jnp.einsum('eai,ebi,abc->ec', xv, ev, W2) * (1.0 / (np.sqrt(3.0) * np.sqrt(MUL1_N * MUL1_E)))
            out_s = (s1 + s2) * inv_sqrt2
            v1 = jnp.einsum('ea,ebi,abc->eci', xs, ev, W3) * (1.0 / np.sqrt(MUL0_N * MUL1_E))
            v2 = jnp.einsum('eai,eb,abc->eci', xv, es, W4) * (1.0 / np.sqrt(MUL1_N * MUL0_E))
            out_v = (v1 + v2) * inv_sqrt2
            return jnp.concatenate([out_s, out_v.reshape(out_v.shape[0], -1)], axis=-1)
        row, col = (edge_index[0], edge_index[1])
        tp = fctp_messages(node_features[col], edge_attr_tensor, W1, W2, W3, W4)
        messages = tp @ Wm + bm
        agg = jax.ops.segment_sum(messages, row, num_segments=N_NODES)
        upd = jnp.concatenate([node_features, agg], axis=-1) @ Wu + bu
        return node_features + upd
    edge_index = jnp.stack([src, dst])
    x = _layernorm(x + _L0_gnn_ref(x, edge_index, edge_attr_32, node_vec1, L0_gnn_W1, L0_gnn_W2, L0_gnn_W3, L0_gnn_W4, L0_gnn_Wm, L0_gnn_bm, L0_gnn_Wu, L0_gnn_bu), axis=-1)
    return x

_drawn_inputs = setup_inputs


def setup_inputs(seed=0):
    import zlib

    import numpy as np

    out = dict(_drawn_inputs(seed))
    spreads = {'L0_gnn_bm': (0.0, 0.1), 'L0_gnn_bu': (0.0, 0.1)}
    factors = {}
    for name, (base, spread) in spreads.items():
        noise = np.random.default_rng([zlib.crc32(name.encode()), seed]).standard_normal(out[name].shape)
        drawn = base * np.exp(spread * noise) if base else spread * noise
        out[name] = jnp.asarray(drawn.astype(out[name].dtype))
    for name, factor in factors.items():
        out[name] = (out[name] * factor).astype(out[name].dtype)
    return out
```

```python
from contextlib import ExitStack

import concourse.bass as bass
from concourse import mybir

F32 = mybir.dt.float32
BF16 = mybir.dt.bfloat16
I32 = mybir.dt.int32
U32 = mybir.dt.uint32
ALU = mybir.AluOpType
ACT = mybir.ActivationFunctionType

P = 128
TILES = 4
GE = P * TILES
D = 160
NS, NV, DE = 64, 32, 32
NQ = 12
NPROD = 22
USES = 7
EPS = 1e-5


def shift(group, by, m=2):
    j, u = group
    return j + (u + by) // m, (u + by) % m


def number(group, m=2):
    return group[0] * m + group[1]


def at_least(group, least, m=2):
    return not isinstance(group[0], int) or number(group, m) >= least


def run_slots(engine, slot, first, last, loop_from, loop_to, m=2):
    assert loop_from % m == 0 and loop_to % m == 0
    for s in range(first, loop_from):
        slot((s // m, s % m))
    with engine.Fori(loop_from // m, loop_to // m) as j:
        for u in range(m):
            slot((j, u))
    for s in range(loop_to, last):
        slot((s // m, s % m))


def build(nc, x, dst_idx, src_idx, src_row, edge_attr, w1, w2, w3, w4, wm_t, wu, bu, ident, select,
          sum_select, lower, trash, out):
    n_nodes = x.shape[0]
    n_groups = dst_idx.shape[0]
    n_rows = (n_nodes + 2 * P - 1) // P * P
    full = n_nodes // GE
    rest = (n_nodes - full * GE) // TILES
    n_out = full + (rest > 0)
    assert rest * TILES + full * GE == n_nodes

    agg = nc.dram_tensor("agg", [n_rows, D], F32, kind="Internal").ap()

    with ExitStack() as ctx:
        def sb(name, shape, dt=F32):
            return ctx.enter_context(nc.sbuf_tensor(name, shape, dt))

        def two(name, shape, dt=F32):
            return [sb(f"{name}{u}", shape, dt) for u in range(2)]

        def sem(name):
            return ctx.enter_context(nc.semaphore(name))

        ident_sb = sb("ident_sb", [P, P])
        ident_bf = sb("ident_bf", [P, P], BF16)
        select_sb = sb("select_sb", [3 * DE, NQ * P], BF16)
        sum_sb = sb("sum_sb", [P, NV])
        lower_sb = sb("lower_sb", [P, P])
        trash_sb = sb("trash_sb", [P, TILES])
        ones_bf = sb("ones_bf", [P, 1], BF16)
        w1_sb = sb("w1_sb", [P, 4, NS])
        w2_sb = sb("w2_sb", [P, 2, NS])
        w3_sb = sb("w3_sb", [P, P])
        w4_sb = sb("w4_sb", [P, 2, NV])
        wc_s = sb("wc_s", [P, D])
        wc_v = sb("wc_v", [97, D])
        wux_a = sb("wux_a", [P, D])
        wux_b = sb("wux_b", [33, D])
        zeros = sb("zeros", [P, 14 * D])
        dst_sb = two("dst_sb", [P, TILES], I32)
        src_sb = two("src_sb", [P, TILES], I32)
        row_sb = two("row_sb", [P, TILES, P], I32)
        e_sb = two("e_sb", [P, TILES, DE])
        e_low = sb("e_low", [P, TILES, DE])
        e3 = two("e3", [P, TILES, 3, DE], BF16)
        xg = two("xg", [P, TILES, D])
        spread = sb("spread", [P, TILES, 4, P])
        eT = two("eT", [3 * DE, GE], BF16)
        XY = two("XY", [P, 6, GE])
        prod = two("prod", [P, NPROD, GE])
        S_sb = two("S_sb", [P, GE])
        V_sb = two("V_sb", [97, GE])
        same = two("same", [P, TILES, P])
        same_low = two("same_low", [P, TILES, P], BF16)
        msg = two("msg", [P, TILES, D])
        summed = two("summed", [P, 2, 2 * D + 2])
        to_trash = sb("to_trash", [P, TILES])
        moved = sb("moved", [P, TILES])
        row_idx = two("row_idx", [P, TILES], I32)
        stage = prod[0][:, :, :].rearrange("p n e -> p (n e)")
        wm_a, wm_b = stage[:, 0:225], stage[0:32, 225:450]
        wu2_a, wu2_b = stage[:, 450:610], stage[0:32, 610:770]
        select_st = stage[0:3 * DE, 1024:1024 + NQ * P]
        nodes = prod[0][:, :, :].rearrange("p n e -> p (n e)")
        nodes2 = prod[1][:, :, :].rearrange("p n e -> p (n e)")
        xn = [nodes[:, b * 640:(b + 1) * 640] for b in range(4)]
        an = [nodes[:, (4 + b) * 640:(5 + b) * 640] for b in range(4)]
        yn = [nodes[:, (8 + b) * 640:(9 + b) * 640] for b in range(4)]
        on = [nodes2[:, b * 640:(b + 1) * 640] for b in range(4)]
        xTa = [nodes2[:, 2560 + b * GE:2560 + (b + 1) * GE] for b in range(2)]
        xTb = [nodes2[0:33, 3584 + b * GE:3584 + (b + 1) * GE] for b in range(2)]
        stats = two("stats", [P, TILES, 6])
        mv = two("mv", [P, TILES, 2])
        eps_sb = sb("eps_sb", [P, 1])
        std = two("std", [P, TILES])
        rstd = two("rstd", [P, TILES])
        shift_n = two("shift_n", [P, TILES])

        ps = ctx.enter_context(nc.psum_tensor("ps", [P, 8, 512], F32))
        M_BANK, S_BANK, V_BANK, T_BANK, E_BANK = 0, 2, 3, 4, 6
        msg_ps = ps[:, M_BANK:M_BANK + 2, 0:2 * D]
        sum_ps = ps[:, M_BANK:M_BANK + 2, 0:2 * D + 2]

        consts_in = sem("consts_in")
        table_zero = sem("table_zero")
        dst_e_in = [sem(f"dst_e_in{u}") for u in range(2)]
        src_in = [sem(f"src_in{u}") for u in range(2)]
        x_gathered = [sem(f"x_gathered{u}") for u in range(2)]
        scattered = sem("scattered")
        nodes_in = [sem(f"nodes_in{b}") for b in range(4)]
        nodes_out = [sem(f"nodes_out{b}") for b in range(4)]
        e_split = sem("e_split")
        same_low_done = sem("same_low_done")
        pool_passed = sem("pool_passed")
        wc_ready = sem("wc_ready")
        t_ready = sem("t_ready")
        e_ready = sem("e_ready")
        S_ready = sem("S_ready")
        V_ready = sem("V_ready")
        msg_ready = sem("msg_ready")
        summed_ready = sem("summed_ready")
        xT_ready = sem("xT_ready")
        upd_ready = sem("upd_ready")
        x_spread = sem("x_spread")
        scaled = sem("scaled")
        t_free = sem("t_free")
        S_copied = sem("S_copied")
        V_copied = sem("V_copied")
        msg_copied = sem("msg_copied")
        summed_copied = sem("summed_copied")
        xT_copied = sem("xT_copied")
        std_done = sem("std_done")
        normed = sem("normed")
        setup_done = sem("setup_done")
        wc_copied = sem("wc_copied")
        multiplied = sem("multiplied")
        same_done = sem("same_done")
        idx_step = sem("idx_step")
        ones_set = sem("ones_set")
        ln_step = sem("ln_step")
        dve_passed = sem("dve_passed")
        rstd_step = sem("rstd_step")

        LN = 9
        DVE_SETUP = 10

        def hold(engine, passed):
            engine.sem_inc(passed, 1)

        block = ctx.enter_context(nc.Block())

        @block.sync
        def _(sp):
            for to, frm in (
                (select_st, select), (wm_a, wm_t[0:P, :]), (wm_b, wm_t[P:D, :]),
                (wu2_a, wu[D:D + P, :]), (wu2_b, wu[D + P:2 * D, :]),
                (ident_sb[:, :], ident), (sum_sb[:, :], sum_select), (lower_sb[:, :], lower),
                (trash_sb[:, :], trash), (wux_a[:, :], wu[0:P, :]), (wux_b[0:32, :], wu[P:D, :]),
                (wux_b[32:33, :], bu), (w3_sb[:, :], w3), (w4_sb[:, :, :], w4),
            ):
                sp.dma_start(to, frm).then_inc(consts_in, 16)
            sp.dma_start(w1_sb[:, :, :], w1).then_inc(consts_in, 16)
            sp.dma_start(w2_sb[:, :, :], w2).then_inc(consts_in, 16)

            def load_dst_e(g):
                if at_least(g, 2):
                    sp.wait_ge(x_gathered[g[1]], g[0] * 64)
                    sp.wait_ge(e_split, number(g) * 4 - 4)
                sp.dma_start(dst_sb[g[1]][:, :], dst_idx[number(g), :, :]).then_inc(dst_e_in[g[1]], 16)
                sp.dma_start(e_sb[g[1]][:, :, :], edge_attr[number(g), :, :, :]).then_inc(dst_e_in[g[1]], 16)

            def load_src(g):
                if at_least(g, 2):
                    sp.wait_ge(idx_step, number(g) * 3 - 3)
                sp.dma_start(src_sb[g[1]][:, :], src_idx[number(g), :, :]).then_inc(src_in[g[1]], 16)
                sp.dma_start(row_sb[g[1]][:, :, :],
                             src_row[number(g), :, :].to_broadcast([P, GE])
                             .rearrange("p (s e) -> p s e", s=TILES)).then_inc(src_in[g[1]], 16)

            def slot(s):
                if not isinstance(s[0], int) or 0 <= number(s) + 3 < n_groups:
                    load_dst_e(shift(s, 3))
                if not isinstance(s[0], int) or 0 <= number(s) < n_groups:
                    load_src(s)

            run_slots(sp, slot, -3, n_groups, 2, (n_groups - 3) // 2 * 2)

            sp.wait_ge(scattered, 16 * TILES * n_groups)

            def load_nodes(c, parts):
                if at_least(c, 4, 4):
                    sp.wait_ge(ln_step, number(c, 4) * LN - 4 * LN + 1)
                b = c[1]
                rows = number(c, 4) * GE
                for to, frm in ((xn[b], x), (an[b], agg)):
                    sp.dma_start(to[0:parts, :],
                                 frm[bass.ds(rows, parts * TILES), :].rearrange("(p s) d -> p (s d)", s=TILES)
                                 ).then_inc(nodes_in[b], 16)

            def store_nodes(c, parts):
                sp.wait_ge(normed, number(c, 4) + 1)
                sp.dma_start(out[bass.ds(number(c, 4) * GE, parts * TILES), :]
                             .rearrange("(p s) d -> p (s d)", s=TILES),
                             on[c[1]][0:parts, :]).then_inc(nodes_out[c[1]], 16)

            def node_slot(c):
                parts = lambda d: rest if isinstance(c[0], int) and number(c, 4) + d == full else P
                if not isinstance(c[0], int) or 0 <= number(c, 4) + 3 < n_out:
                    load_nodes(shift(c, 3, 4), parts(3))
                if at_least(c, 0, 4):
                    store_nodes(c, parts(0))

            run_slots(sp, node_slot, -3, n_out, 4, (full - 3) // 4 * 4, 4)
            for b in range(4):
                sp.wait_ge(nodes_out[b], 16 * ((n_out - b + 3) // 4))

        @block.gpsimd
        def _(pool):
            def gather(g, q):
                if q == 0:
                    pool.wait_ge(dst_e_in[g[1]], g[0] * 32 + 32)
                    if at_least(g, 2):
                        pool.wait_ge(x_spread, number(g) * 4 - 4)
                hold(pool, pool_passed)
                nc.gpsimd.indirect_dma_start(
                    xg[g[1]][:, q, :], None, x,
                    bass.IndirectOffsetOnAxis(dst_sb[g[1]][:, q:q + 1].bitcast(U32), 0)
                ).then_inc(x_gathered[g[1]], 16)

            def split(g, step):
                high, mid, low = (e3[g[1]][:, :, k, :] for k in range(3))
                if step == 0:
                    pool.wait_ge(dst_e_in[g[1]], g[0] * 32 + 32)
                    if at_least(g, 2):
                        pool.wait_ge(t_ready, number(g) * USES - 2 * USES + 5)
                    if at_least(g, 1):
                        pool.wait_ge(e_split, number(g) * 4)
                    hold(pool, pool_passed)
                    nc.gpsimd.tensor_copy(high, e_sb[g[1]][:, :, :]).then_inc(e_split, 1)
                    return
                pool.wait_ge(e_split, number(g) * 4 + step)
                if step == 1:
                    nc.gpsimd.tensor_tensor(e_low[:, :, :], e_sb[g[1]][:, :, :], high, ALU.subtract).then_inc(e_split, 1)
                elif step == 2:
                    hold(pool, pool_passed)
                    nc.gpsimd.tensor_copy(mid, e_low[:, :, :]).then_inc(e_split, 1)
                else:
                    nc.gpsimd.tensor_tensor(low, e_low[:, :, :], mid, ALU.subtract).then_inc(e_split, 1)

            def mask_same(g):
                pool.wait_ge(same_done, number(g) + 1)
                if at_least(g, 2):
                    pool.wait_ge(summed_ready, number(g) - 1)
                nc.gpsimd.tensor_tensor(same_low[g[1]][:, :, :], same[g[1]][:, :, :],
                                        lower_sb[:, :].unsqueeze(1).to_broadcast([P, TILES, P]),
                                        ALU.mult).then_inc(same_low_done, 1)

            def scatter(g, q):
                if q == 0:
                    pool.wait_ge(summed_copied, number(g) + 1)
                    pool.wait_ge(idx_step, number(g) * 3 + 3)
                if at_least(g, 1) or q:
                    pool.wait_ge(scattered, number(g) * 64 + q * 16)
                else:
                    pool.wait_ge(table_zero, 16)
                hold(pool, pool_passed)
                nc.gpsimd.indirect_dma_start(
                    agg, bass.IndirectOffsetOnAxis(row_idx[g[1]][:, q:q + 1].bitcast(U32), 0),
                    summed[g[1]][:, q // 2, q % 2 * D:(q % 2 + 1) * D], None, compute_op=ALU.add).then_inc(scattered, 16)

            pool.wait_ge(consts_in, 16 * 16)

            def slot(s):
                live = lambda d: not isinstance(s[0], int) or 0 <= number(s) + d < n_groups
                for q in range(TILES):
                    if live(-3):
                        scatter(shift(s, -3), q)
                    if live(2):
                        gather(shift(s, 2), q)
                        split(shift(s, 2), q)
                    if q == 1 and live(-1):
                        mask_same(shift(s, -1))

            run_slots(pool, slot, -2, n_groups + 3, 4, (n_groups - 2) // 2 * 2)

        @block.scalar
        def _(act):
            act.wait_ge(setup_done, 1)
            act.dma_start(agg.rearrange("(p k r) d -> p k (r d)", p=P, r=14),
                          zeros[:, :].unsqueeze(1).to_broadcast([P, n_rows // P // 14, 14 * D])).then_inc(table_zero, 16)
            act.wait_ge(consts_in, 16 * 16)
            half = 0.5 ** 0.5
            nc.scalar.mul(w1_sb[:, :, :], w1_sb[:, :, :], half / (64 * 8) ** 0.5).then_inc(scaled, 1)
            nc.scalar.mul(w2_sb[:, :, :], w2_sb[:, :, :], half / (3 * 32 * 8) ** 0.5).then_inc(scaled, 1)
            nc.scalar.mul(w3_sb[:, :], w3_sb[:, :], half / (64 * 8) ** 0.5).then_inc(scaled, 1)
            nc.scalar.mul(w4_sb[:, :, :], w4_sb[:, :, :], half / (32 * 8) ** 0.5).then_inc(scaled, 1)
            act.sem_inc(t_free, 2)

            def spread_x(g, k):
                if k == 0:
                    act.wait_ge(x_gathered[g[1]], g[0] * 64 + 64)
                    if at_least(g, 1):
                        act.wait_ge(t_ready, number(g) * USES - USES + 4)
                    frm = xg[g[1]][:, :, 0:NS].unsqueeze(2).to_broadcast([P, TILES, 2, NS])
                    to = spread[:, :, 0, :].rearrange("p q (r a) -> p q r a", r=2)
                else:
                    frm = xg[g[1]][:, :, NS + k - 1:D:3].unsqueeze(2).to_broadcast([P, TILES, 4, NV])
                    to = spread[:, :, k, :].rearrange("p q (r a) -> p q r a", r=4)
                nc.scalar.activation(to, frm, ACT.Copy).then_inc(x_spread, 1)

            def evacuate(g, k):
                if k == 0 and at_least(g, 2):
                    act.wait_ge(multiplied, number(g) * NQ - NQ + 2)
                act.wait_ge(t_ready, number(g) * USES + k + 1)
                bank = ps[:, T_BANK + (g[1] * USES + k) % 2, :]
                if k == 4:
                    to, frm = eT[g[1]][:, :], bank.bitcast(BF16)[0:3 * DE, 0:GE]
                else:
                    to, frm = XY[g[1]][:, k if k < 4 else k - 1, :], bank
                nc.scalar.activation(to, frm, ACT.Copy).then_inc(t_free, 1)

            def copy_S(g):
                act.wait_ge(S_ready, number(g) + 1)
                if at_least(g, 2):
                    act.wait_ge(msg_ready, number(g) - 1)
                nc.scalar.activation(S_sb[g[1]][:, :], ps[:, S_BANK, :], ACT.Copy).then_inc(S_copied, 1)

            def copy_V(g):
                act.wait_ge(V_ready, number(g) + 1)
                if at_least(g, 2):
                    act.wait_ge(msg_ready, number(g) - 1)
                nc.scalar.activation(V_sb[g[1]][0:96, :], ps[0:96, V_BANK, :], ACT.Copy).then_inc(V_copied, 1)

            def copy_msg(g):
                act.wait_ge(msg_ready, number(g) + 1)
                if at_least(g, 2):
                    act.wait_ge(summed_ready, number(g) - 1)
                nc.scalar.activation(msg[g[1]][:, :, :].rearrange("p (a b) d -> p a (b d)", a=2), msg_ps,
                                     ACT.Copy).then_inc(msg_copied, 1)

            def copy_summed(g):
                act.wait_ge(summed_ready, number(g) + 1)
                if at_least(g, 2):
                    act.wait_ge(scattered, number(g) * 64 - 64)
                nc.scalar.activation(summed[g[1]][:, :, :], sum_ps, ACT.Copy).then_inc(summed_copied, 1)

            def slot(s):
                live = lambda d: not isinstance(s[0], int) or 0 <= number(s) + d < n_groups
                if live(1):
                    for k in range(4):
                        spread_x(shift(s, 1), k)
                if live(-2):
                    copy_msg(shift(s, -2))
                    copy_summed(shift(s, -2))
                if live(-1):
                    copy_S(shift(s, -1))
                if live(1):
                    for k in range(USES):
                        evacuate(shift(s, 1), k)
                if live(-1):
                    copy_V(shift(s, -1))

            run_slots(act, slot, -1, n_groups + 2, 4, (n_groups - 1) // 2 * 2)

            def node_slot(c):
                n, b = number(c, 4), c[1]
                parts = rest if isinstance(n, int) and n == full else P
                if not isinstance(n, int) or n < n_out:
                    act.wait_ge(xT_ready, n + 1)
                    if at_least(c, 2, 4):
                        act.wait_ge(upd_ready, n - 1)
                    nc.scalar.activation(xTa[b % 2].rearrange("k (s p) -> k s p", s=TILES)[:, :, 0:parts],
                                         ps[:, 4 + b % 2, :].rearrange("k (s p) -> k s p", s=TILES)[:, :, 0:parts],
                                         ACT.Copy).then_inc(xT_copied, 1)
                    nc.scalar.activation(xTb[b % 2][0:32].rearrange("k (s p) -> k s p", s=TILES)[:, :, 0:parts],
                                         ps[0:32, 6 + b % 2, :].rearrange("k (s p) -> k s p", s=TILES)[:, :, 0:parts],
                                         ACT.Copy).then_inc(xT_copied, 1)
                if at_least(c, 1, 4) and not (isinstance(n, int) and n > n_out):
                    d = shift(c, -1, 4)
                    m, v = number(d, 4), d[1] % 2
                    parts = rest if isinstance(m, int) and m == full else P
                    act.wait_ge(ln_step, m * LN + LN)
                    if at_least(d, 2, 4):
                        act.wait_ge(rstd_step, m * 2 - 2)
                    nc.scalar.activation(std[v][0:parts], mv[v][0:parts, :, 1], ACT.Sqrt,
                                         bias=eps_sb[0:parts, :]).then_inc(std_done, 1)
                if at_least(c, 2, 4):
                    c = shift(c, -2, 4)
                    n, b = number(c, 4), c[1]
                    parts = rest if isinstance(n, int) and n == full else P
                    act.wait_ge(rstd_step, n * 2 + 2)
                    if at_least(c, 4, 4):
                        act.wait_ge(nodes_out[b], c[0] * 16)
                    for q in range(TILES):
                        last = nc.scalar.activation(on[b][0:parts, q * D:(q + 1) * D], yn[b][0:parts, q * D:(q + 1) * D],
                                                    ACT.Identity, bias=shift_n[b % 2][0:parts, q:q + 1],
                                                    scale=rstd[b % 2][0:parts, q:q + 1])
                    last.then_inc(normed, 1)

            run_slots(act, node_slot, 0, n_out + 2, 8, full // 4 * 4, 4)

        @block.vector
        def _(dve):
            nc.vector.memset(zeros[:, :], 0.0).then_inc(setup_done, 1)
            nc.vector.memset(ones_bf[:, :], 1.0).then_inc(setup_done, 1)
            nc.vector.memset(eps_sb[:, :], EPS).then_inc(setup_done, 1)
            for u in range(2):
                nc.vector.memset(V_sb[u][96:97, :], 1.0).then_inc(setup_done, 1)
            dve.wait_ge(consts_in, 16 * 16)
            nc.vector.tensor_copy(ident_bf[:, :], ident_sb[:, :]).then_inc(setup_done, 1)
            nc.vector.tensor_copy(select_sb[:, :], select_st).then_inc(setup_done, 1)
            nc.vector.scalar_tensor_tensor(wux_a[:, 0:P], ident_sb[:, :], 2.0, wux_a[:, 0:P],
                                           ALU.mult, ALU.add).then_inc(setup_done, 1)
            nc.vector.scalar_tensor_tensor(wux_b[0:32, P:D], ident_sb[0:32, 0:32], 2.0, wux_b[0:32, P:D],
                                           ALU.mult, ALU.add).then_inc(setup_done, 1)
            dve.wait_ge(wc_ready, 1)
            nc.vector.tensor_copy(wc_s[:, :], ps[:, M_BANK, 0:D]).then_inc(wc_copied, 1)
            nc.vector.tensor_copy(wc_v[:, :], ps[0:97, M_BANK + 1, 0:D]).then_inc(wc_copied, 1)
            dve.wait_ge(setup_done, DVE_SETUP - 1)
            nc.vector.memset(to_trash[:, :], 0.0).then_inc(setup_done, 1)
            dve.sem_inc(multiplied, 2)

            def multiply(g, q):
                if q == 0:
                    if at_least(g, 2):
                        dve.wait_ge(S_ready, number(g) - 1)
                        dve.wait_ge(V_ready, number(g) - 1)
                    dve.wait_ge(t_free, number(g) * USES + 6)
                if q == 6:
                    dve.wait_ge(t_free, number(g) * USES + 9)
                dve.wait_ge(e_ready, number(g) * NQ + q + 1)
                tiles = XY[g[1]]
                if q < 4:
                    count, first, frm = 1, q, tiles[:, 0:1, :]
                elif q < 6:
                    count, first, frm = 3, 4 + 3 * (q - 4), tiles[:, 1:4, :]
                else:
                    fours, i = divmod(q - 6, 3)
                    step = 4 + fours - (1 + i)
                    count, first, frm = 2, 10 + 2 * (q - 6), tiles[:, 1 + i:4 + fours + 1:step, :]
                edge = ps[:, E_BANK + q % 2, :].unsqueeze(1).to_broadcast([P, count, GE])
                nc.vector.tensor_tensor(prod[g[1]][:, first:first + count, :], frm, edge,
                                        ALU.mult).then_inc(multiplied, 1)

            def find_same(g):
                dve.wait_ge(src_in[g[1]], g[0] * 32 + 32)
                if at_least(g, 2):
                    dve.wait_ge(summed_ready, number(g) - 1)
                nc.vector.tensor_tensor(same[g[1]][:, :, :], row_sb[g[1]][:, :, :],
                                        src_sb[g[1]][:, :].unsqueeze(2).to_broadcast([P, TILES, P]),
                                        ALU.is_equal).then_inc(same_done, 1)

            def rows(g):
                n = number(g)
                if at_least(g, 1):
                    dve.wait_ge(idx_step, n * 3)
                dve.wait_ge(src_in[g[1]], g[0] * 32 + 32)
                nc.vector.tensor_tensor(to_trash[:, :], trash_sb[:, :], src_sb[g[1]][:, :],
                                        ALU.subtract).then_inc(idx_step, 1)
                dve.wait_ge(idx_step, n * 3 + 1)
                dve.wait_ge(summed_copied, n + 1)
                nc.vector.scalar_tensor_tensor(moved[:, :].rearrange("p (a b) -> p a b", a=2),
                                               summed[g[1]][:, :, 2 * D:2 * D + 2], 1.0,
                                               to_trash[:, :].rearrange("p (a b) -> p a b", a=2),
                                               ALU.min, ALU.mult).then_inc(idx_step, 1)
                dve.wait_ge(idx_step, n * 3 + 2)
                if at_least(g, 2):
                    dve.wait_ge(scattered, n * 64 - 64)
                nc.vector.tensor_tensor(row_idx[g[1]][:, :], moved[:, :], src_sb[g[1]][:, :],
                                        ALU.add).then_inc(idx_step, 1)

            dve.wait_ge(setup_done, DVE_SETUP)

            def slot(s):
                live = lambda d: not isinstance(s[0], int) or 0 <= number(s) + d < n_groups
                for q in range(NQ):
                    if live(0):
                        multiply(s, q)
                    if q == 2 and live(-1):
                        find_same(shift(s, -1))
                    if q == 7 and live(-2):
                        rows(shift(s, -2))

            run_slots(dve, slot, 0, n_groups + 2, 4, n_groups // 2 * 2)

            dve.wait_ge(scattered, 16 * TILES * n_groups)
            for b in range(2):
                nc.vector.memset(xTb[b][32:33, :], 1.0).then_inc(ones_set, 1)

            def node_slot(c):
                n, b = number(c, 4), c[1]
                parts = rest if isinstance(n, int) and n == full else P
                if not isinstance(n, int) or n < n_out:
                    dve.wait_ge(upd_ready, n + 1)
                    dve.wait_ge(nodes_in[b], c[0] * 32 + 32)
                    if at_least(c, 4, 4):
                        dve.wait_ge(normed, n - 3)
                    y, st, m = yn[b][0:parts], stats[b % 2][0:parts], mv[b % 2][0:parts]
                    nc.vector.tensor_tensor(y.rearrange("p (a e) -> p a e", a=2),
                                            ps[0:parts, 2 * (b % 2):2 * (b % 2) + 2, 0:2 * D],
                                            an[b][0:parts].rearrange("p (a e) -> p a e", a=2),
                                            ALU.add).then_inc(ln_step, 1)
                if at_least(c, 1, 4):
                    d = shift(c, -1, 4)
                    k, v = number(d, 4), d[1] % 2
                    some = rest if isinstance(k, int) and k == full else P
                    dve.wait_ge(std_done, k + 1)
                    if at_least(d, 2, 4):
                        dve.wait_ge(normed, k - 1)
                    nc.vector.reciprocal(rstd[v][0:some], std[v][0:some]).then_inc(rstd_step, 1)
                    dve.wait_ge(rstd_step, k * 2 + 1)
                    nc.vector.scalar_tensor_tensor(shift_n[v][0:some], mv[v][0:some, :, 0], -1.0,
                                                   rstd[v][0:some], ALU.mult, ALU.mult).then_inc(rstd_step, 1)
                if not isinstance(n, int) or n < n_out:
                    dve.wait_ge(ln_step, n * LN + 1)
                    for q in range(TILES):
                        nc.vector.bn_stats(st[:, q, :], y[:, q * D:(q + 1) * D]).then_inc(ln_step, 1)
                    if at_least(c, 2, 4):
                        dve.wait_ge(rstd_step, n * 2 - 2)
                    for q in range(TILES):
                        dve.wait_ge(ln_step, n * LN + 2 + q)
                        hold(dve, dve_passed)
                        nc.vector.bn_aggr(m[:, q, :], st[:, q, :]).then_inc(ln_step, 1)

            run_slots(dve, node_slot, 0, n_out + 1, 4, full // 4 * 4, 4)

        @block.tensor
        def _(pe):
            pe.wait_ge(consts_in, 16 * 16)
            nc.tensor.matmul(ps[:, M_BANK, 0:D], wm_a[:, 0:P], wu2_a, start=True, stop=False)
            nc.tensor.matmul(ps[:, M_BANK, 0:D], wm_b[:, 0:P], wu2_b, start=False, stop=True)
            nc.tensor.matmul(ps[0:97, M_BANK + 1, 0:D], wm_a[:, P:225], wu2_a, start=True, stop=False)
            nc.tensor.matmul(ps[0:97, M_BANK + 1, 0:D], wm_b[:, P:225], wu2_b, start=False,
                             stop=True).then_inc(wc_ready, 1)
            pe.wait_ge(wc_copied, 2)
            pe.wait_ge(setup_done, DVE_SETUP)
            pe.wait_ge(scaled, 4)

            def bank_free(g, k):
                pe.wait_ge(t_free, number(g) * USES + k + 1)

            def transpose_x(g, k):
                pe.wait_ge(x_spread, number(g) * 4 + k + 1)
                bank_free(g, k)
                for q in range(TILES):
                    last = nc.tensor.transpose(ps[:, T_BANK + (g[1] * USES + k) % 2, q * P:(q + 1) * P],
                                               spread[:, q, k, :], ident_sb[:, :])
                last.then_inc(t_ready, 1)

            def transpose_e(g):
                pe.wait_ge(e_split, number(g) * 4 + 4)
                bank_free(g, 4)
                bank = ps[:, T_BANK + (g[1] * USES + 4) % 2, :].bitcast(BF16)
                for q in range(TILES):
                    last = nc.tensor.transpose(bank[0:3 * DE, q * P:(q + 1) * P],
                                               e3[g[1]][:, q, :, :].rearrange("p k c -> p (k c)"), ident_bf[:, :])
                last.then_inc(t_ready, 1)

            def times_w3(g):
                for h in range(2):
                    bank_free(g, 5 + h)
                    nc.tensor.matmul(ps[:, T_BANK + (g[1] * USES + 5 + h) % 2, :], w3_sb[64 * h:64 * h + 64, :],
                                     XY[g[1]][64 * h:64 * h + 64, 0, :], start=True, stop=True).then_inc(t_ready, 1)

            def replicate(g, q):
                if q == 0:
                    pe.wait_ge(t_free, number(g) * USES + 7)
                pe.wait_ge(multiplied, number(g) * NQ + q + 1)
                nc.tensor.matmul(ps[:, E_BANK + q % 2, :], select_sb[:, q * P:(q + 1) * P], eT[g[1]][:, :],
                                 start=True, stop=True).then_inc(e_ready, 1)

            def contract_S(g, n):
                if n == 0:
                    pe.wait_ge(multiplied, number(g) * NQ + NQ + 2)
                    if at_least(g, 1):
                        pe.wait_ge(S_copied, number(g))
                for h in range(2):
                    k = 2 * n + h
                    tile, w = (k, w1_sb[:, k, :]) if k < 4 else (10 + 2 * (k - 4), w2_sb[:, (k - 4) // 3, :])
                    last = nc.tensor.matmul(ps[64 * h:64 * h + 64, S_BANK, :], w, prod[g[1]][:, tile, :],
                                            start=n == 0, stop=n == 4)
                if n == 4:
                    last.then_inc(S_ready, 1)

            def contract_V(g, n):
                if n == 0 and at_least(g, 1):
                    pe.wait_ge(V_copied, number(g))
                for i in range(3):
                    tile, w = (4 + 3 * n + i, w4_sb[:, n, :]) if n < 2 else (11 + 2 * (3 * (n - 2) + i), sum_sb[:, :])
                    last = nc.tensor.matmul(ps[32 * i:32 * i + 32, V_BANK, :], w, prod[g[1]][:, tile, :],
                                            start=n == 0, stop=n == 3)
                if n == 3:
                    last.then_inc(V_ready, 1)

            def messages(g):
                pe.wait_ge(S_copied, number(g) + 1)
                pe.wait_ge(V_copied, number(g) + 1)
                if at_least(g, 1):
                    pe.wait_ge(summed_copied, number(g))
                for q in range(TILES):
                    to = msg_ps[:, q // 2, q % 2 * D:(q % 2 + 1) * D]
                    nc.tensor.matmul(to, S_sb[g[1]][:, q * P:(q + 1) * P], wc_s[:, :], start=True, stop=False)
                    last = nc.tensor.matmul(to, V_sb[g[1]][:, q * P:(q + 1) * P], wc_v[:, :], start=False, stop=True)
                last.then_inc(msg_ready, 1)

            def sum_same(g):
                pe.wait_ge(msg_copied, number(g) + 1)
                pe.wait_ge(same_done, number(g) + 1)
                pe.wait_ge(same_low_done, number(g) + 1)
                for q in range(TILES):
                    nc.tensor.matmul(msg_ps[:, q // 2, q % 2 * D:(q % 2 + 1) * D], same[g[1]][:, q, :],
                                     msg[g[1]][:, q, :], start=True, stop=True)
                for q in range(TILES):
                    last = nc.tensor.matmul(sum_ps[:, q // 2, 2 * D + q % 2:2 * D + q % 2 + 1], same_low[g[1]][:, q, :], ones_bf[:, :],
                                            start=True, stop=True)
                last.then_inc(summed_ready, 1)

            def slot(s):
                live = lambda d: not isinstance(s[0], int) or 0 <= number(s) + d < n_groups
                before, two_before, after = shift(s, -1), shift(s, -2), shift(s, 1)
                for q in range(NQ):
                    if live(0):
                        replicate(s, q)
                    if live(-2) and q == 1:
                        messages(two_before)
                    if live(-2) and q == 4:
                        sum_same(two_before)
                    if live(-1) and q in (2, 3, 5, 6, 7):
                        contract_S(before, (2, 3, 5, 6, 7).index(q))
                    if live(1) and q == 7:
                        transpose_x(after, 0)
                        transpose_x(after, 1)
                    if live(1) and q == 8:
                        transpose_x(after, 2)
                        transpose_x(after, 3)
                    if live(1) and q == 9:
                        transpose_e(after)
                    if live(1) and q == 10:
                        times_w3(after)
                    if live(-1) and q >= 8:
                        contract_V(before, q - 8)

            run_slots(pe, slot, -1, n_groups + 2, 4, (n_groups - 1) // 2 * 2)

            pe.wait_ge(scattered, 16 * TILES * n_groups)
            pe.wait_ge(ones_set, 2)

            def node_slot(c):
                n, b = number(c, 4), c[1]
                if not isinstance(n, int) or n < n_out:
                    parts = rest if isinstance(n, int) and n == full else P
                    pe.wait_ge(nodes_in[b], c[0] * 32 + 32)
                    if at_least(c, 2, 4):
                        pe.wait_ge(xT_copied, n * 2 - 2)
                    for q in range(TILES):
                        row = xn[b][0:parts, q * D:(q + 1) * D]
                        nc.tensor.transpose(ps[:, 4 + b % 2, q * P:q * P + parts], row[:, 0:P],
                                            ident_sb[0:parts, 0:parts])
                        last = nc.tensor.transpose(ps[0:32, 6 + b % 2, q * P:q * P + parts], row[:, P:D],
                                                   ident_sb[0:parts, 0:parts])
                    last.then_inc(xT_ready, 1)
                if at_least(c, 1, 4):
                    c = shift(c, -1, 4)
                    n, b = number(c, 4), c[1]
                    parts = rest if isinstance(n, int) and n == full else P
                    pe.wait_ge(xT_copied, n * 2 + 2)
                    if at_least(c, 2, 4):
                        pe.wait_ge(ln_step, n * LN - 2 * LN + 1)
                    for q in range(TILES):
                        to = ps[0:parts, 2 * (b % 2) + q // 2, q % 2 * D:(q % 2 + 1) * D]
                        nc.tensor.matmul(to, xTa[b % 2][:, q * P:q * P + parts], wux_a[:, :], start=True, stop=False)
                        last = nc.tensor.matmul(to, xTb[b % 2][:, q * P:q * P + parts], wux_b[:, :],
                                                start=False, stop=True)
                    last.then_inc(upd_ready, 1)

            run_slots(pe, node_slot, 0, n_out + 1, 4, full // 4 * 4, 4)


def constants(n_nodes):
    import numpy as np

    r = np.arange(P)
    component = np.zeros((NQ, P), np.int64)
    for k in range(4):
        component[k] = 2 * k + r // 64
    for f in range(2):
        component[4 + f] = 4 * f + r // 32
        for i in range(3):
            component[6 + 3 * f + i] = 8 + 3 * (4 * f + r // 32) + i
    select = (np.arange(3 * DE)[:, None] % DE == component.reshape(1, -1)).astype(np.float32)
    sum_select = (r[:, None] % NV == np.arange(NV)[None, :]).astype(np.float32)
    lower = (r[:, None] < r[None, :]).astype(np.float32)
    trash = np.repeat((n_nodes + r)[:, None], TILES, 1).astype(np.float32)
    return {"ident": np.eye(P, dtype=np.float32), "select": select, "sum_select": sum_select,
            "lower": lower, "trash": trash}


def kernel(x, src, dst, edge_attr_32, node_vec1, L0_gnn_W1, L0_gnn_W2, L0_gnn_W3, L0_gnn_W4,
           L0_gnn_Wm, L0_gnn_bm, L0_gnn_Wu, L0_gnn_bu):
    import numpy as np
    import concourse.bacc as bacc
    from concourse.bass_utils import run_bass_kernel_spmd

    x, src, dst, e = (np.asarray(a) for a in (x, src, dst, edge_attr_32))
    W1, W2, W3, W4, Wm, bm, Wu, bu = (np.asarray(a) for a in (
        L0_gnn_W1, L0_gnn_W2, L0_gnn_W3, L0_gnn_W4, L0_gnn_Wm, L0_gnn_bm, L0_gnn_Wu, L0_gnn_bu))
    n_nodes, n_edges = x.shape[0], src.shape[0]
    groups = (n_edges + GE - 1) // GE
    pad = groups * GE - n_edges
    src_p = np.concatenate([src, np.full(pad, n_nodes, src.dtype)])
    dst_p = np.concatenate([dst, np.zeros(pad, dst.dtype)])
    e_p = np.concatenate([e, np.zeros((pad, DE), e.dtype)])
    vec = 64 + 3 * np.arange(NV)[None, :] + np.arange(3)[:, None]
    rows = np.concatenate([Wm[0:64], Wm[0:64], Wm[vec.reshape(-1)], bm[None, :]])
    arrays = {
        "x": x,
        "dst_idx": dst_p.reshape(groups, P, TILES),
        "src_idx": src_p.reshape(groups, P, TILES),
        "src_row": src_p.reshape(groups, P, TILES).transpose(0, 2, 1).reshape(groups, 1, GE),
        "edge_attr": e_p.reshape(groups, P, TILES, DE),
        "w1": W1.transpose(1, 0, 2).reshape(4, P, NS).transpose(1, 0, 2),
        "w2": W2.transpose(1, 0, 2).reshape(2, P, NS).transpose(1, 0, 2),
        "w3": W3.reshape(64, 2, P).transpose(1, 0, 2).reshape(P, P),
        "w4": W4.transpose(1, 0, 2).reshape(2, P, NV).transpose(1, 0, 2),
        "wm_t": rows.T,
        "wu": Wu,
        "bu": bu.reshape(1, D),
        **constants(n_nodes),
    }
    nc = bacc.Bacc("TRN2", target_bir_lowering=False, num_devices=1)
    feeds, aps = {}, []
    for name, a in arrays.items():
        a = np.ascontiguousarray(a)
        feeds[f"in_{name}"] = a
        aps.append(nc.dram_tensor(f"in_{name}", a.shape, mybir.dt.from_np(a.dtype), kind="ExternalInput").ap())
    out = nc.dram_tensor("out", [n_nodes, D], F32, kind="ExternalOutput").ap()
    build(nc, *aps, out)
    result = run_bass_kernel_spmd(nc, [feeds], core_ids=[0])
    return result.results[0]["out"]
```

```python
from contextlib import ExitStack

import concourse.bass as bass
from concourse import mybir

F32 = mybir.dt.float32
BF16 = mybir.dt.bfloat16
I32 = mybir.dt.int32
U32 = mybir.dt.uint32
ALU = mybir.AluOpType
ACT = mybir.ActivationFunctionType

P = 128
TILES = 4
GE = P * TILES
D = 160
NS, NV, DE = 64, 32, 32
NQ = 12
NPROD = 22
USES = 7
EPS = 1e-5


def shift(group, by, m=2):
    j, u = group
    return j + (u + by) // m, (u + by) % m


def number(group, m=2):
    return group[0] * m + group[1]


def at_least(group, least, m=2):
    return not isinstance(group[0], int) or number(group, m) >= least


def run_slots(engine, slot, first, last, loop_from, loop_to, m=2):
    assert loop_from % m == 0 and loop_to % m == 0
    for s in range(first, loop_from):
        slot((s // m, s % m))
    with engine.Fori(loop_from // m, loop_to // m) as j:
        for u in range(m):
            slot((j, u))
    for s in range(loop_to, last):
        slot((s // m, s % m))


def build(nc, x, dst_idx, src_idx, src_row, edge_attr, w1, w2, w3, w4, wm_t, wu, bu, ident, select,
          sum_select, lower, trash, out):
    n_nodes = x.shape[0]
    n_groups = dst_idx.shape[0]
    n_rows = (n_nodes + 2 * P - 1) // P * P
    full = n_nodes // GE
    rest = (n_nodes - full * GE) // TILES
    n_out = full + (rest > 0)
    assert rest * TILES + full * GE == n_nodes

    agg = nc.dram_tensor("agg", [n_rows, D], F32, kind="Internal").ap()

    with ExitStack() as ctx:
        def sb(name, shape, dt=F32):
            return ctx.enter_context(nc.sbuf_tensor(name, shape, dt))

        def two(name, shape, dt=F32):
            return [sb(f"{name}{u}", shape, dt) for u in range(2)]

        def sem(name):
            return ctx.enter_context(nc.semaphore(name))

        ident_sb = sb("ident_sb", [P, P])
        ident_bf = sb("ident_bf", [P, P], BF16)
        select_sb = sb("select_sb", [3 * DE, NQ * P], BF16)
        sum_sb = sb("sum_sb", [P, NV])
        lower_sb = sb("lower_sb", [P, P])
        trash_sb = sb("trash_sb", [P, TILES])
        ones_bf = sb("ones_bf", [P, 1], BF16)
        w1_sb = sb("w1_sb", [P, 4, NS])
        w2_sb = sb("w2_sb", [P, 2, NS])
        w3_sb = sb("w3_sb", [P, P])
        w4_sb = sb("w4_sb", [P, 2, NV])
        wc_s = sb("wc_s", [P, D])
        wc_v = sb("wc_v", [97, D])
        wux_a = sb("wux_a", [P, D])
        wux_b = sb("wux_b", [33, D])
        zeros = sb("zeros", [P, 14 * D])
        dst_sb = two("dst_sb", [P, TILES], I32)
        src_sb = two("src_sb", [P, TILES], I32)
        row_sb = two("row_sb", [P, TILES, P], I32)
        e_sb = two("e_sb", [P, TILES, DE])
        e_low = sb("e_low", [P, TILES, DE])
        e3 = two("e3", [P, TILES, 3, DE], BF16)
        xg = two("xg", [P, TILES, D])
        spread = sb("spread", [P, TILES, 4, P])
        eT = two("eT", [3 * DE, GE], BF16)
        XY = two("XY", [P, 6, GE])
        prod = two("prod", [P, NPROD, GE])
        S_sb = two("S_sb", [P, GE])
        V_sb = two("V_sb", [97, GE])
        same = two("same", [P, TILES, P])
        same_low = two("same_low", [P, TILES, P], BF16)
        msg = two("msg", [P, TILES, D])
        summed = two("summed", [P, 2, 2 * D + 2])
        to_trash = sb("to_trash", [P, TILES])
        moved = sb("moved", [P, TILES])
        row_idx = two("row_idx", [P, TILES], I32)
        stage = prod[0][:, :, :].rearrange("p n e -> p (n e)")
        wm_a, wm_b = stage[:, 0:225], stage[0:32, 225:450]
        wu2_a, wu2_b = stage[:, 450:610], stage[0:32, 610:770]
        select_st = stage[0:3 * DE, 1024:1024 + NQ * P]
        nodes = prod[0][:, :, :].rearrange("p n e -> p (n e)")
        nodes2 = prod[1][:, :, :].rearrange("p n e -> p (n e)")
        xn = [nodes[:, b * 640:(b + 1) * 640] for b in range(4)]
        an = [nodes[:, (4 + b) * 640:(5 + b) * 640] for b in range(4)]
        yn = [nodes[:, (8 + b) * 640:(9 + b) * 640] for b in range(4)]
        on = [nodes2[:, b * 640:(b + 1) * 640] for b in range(4)]
        xTa = [nodes2[:, 2560 + b * GE:2560 + (b + 1) * GE] for b in range(2)]
        xTb = [nodes2[0:33, 3584 + b * GE:3584 + (b + 1) * GE] for b in range(2)]
        stats = two("stats", [P, TILES, 6])
        mv = two("mv", [P, TILES, 2])
        eps_sb = sb("eps_sb", [P, 1])
        std = two("std", [P, TILES])
        rstd = two("rstd", [P, TILES])
        shift_n = two("shift_n", [P, TILES])

        ps = ctx.enter_context(nc.psum_tensor("ps", [P, 8, 512], F32))
        M_BANK, S_BANK, V_BANK, T_BANK, E_BANK = 0, 2, 3, 4, 6
        msg_ps = ps[:, M_BANK:M_BANK + 2, 0:2 * D]
        sum_ps = ps[:, M_BANK:M_BANK + 2, 0:2 * D + 2]

        consts_in = sem("consts_in")
        table_zero = sem("table_zero")
        dst_e_in = [sem(f"dst_e_in{u}") for u in range(2)]
        src_in = [sem(f"src_in{u}") for u in range(2)]
        x_gathered = [sem(f"x_gathered{u}") for u in range(2)]
        scattered = sem("scattered")
        nodes_in = [sem(f"nodes_in{b}") for b in range(4)]
        nodes_out = [sem(f"nodes_out{b}") for b in range(4)]
        e_rests = sem("e_rests")
        parts_added_pool = sem("parts_added_pool")
        same_low_done = sem("same_low_done")
        pool_passed = sem("pool_passed")
        wc_ready = sem("wc_ready")
        t_ready = sem("t_ready")
        e_ready = sem("e_ready")
        S_ready = sem("S_ready")
        V_ready = sem("V_ready")
        msg_ready = sem("msg_ready")
        summed_ready = sem("summed_ready")
        xT_ready = sem("xT_ready")
        upd_ready = sem("upd_ready")
        x_spread = sem("x_spread")
        e_rounded = sem("e_rounded")
        scaled = sem("scaled")
        t_free = sem("t_free")
        S_copied = sem("S_copied")
        V_copied = sem("V_copied")
        msg_copied = sem("msg_copied")
        summed_copied = sem("summed_copied")
        xT_copied = sem("xT_copied")
        std_done = sem("std_done")
        normed = sem("normed")
        setup_done = sem("setup_done")
        wc_copied = sem("wc_copied")
        multiplied = sem("multiplied")
        parts_added_dve = sem("parts_added_dve")
        same_done = sem("same_done")
        idx_step = sem("idx_step")
        ones_set = sem("ones_set")
        ln_step = sem("ln_step")
        dve_passed = sem("dve_passed")
        rstd_step = sem("rstd_step")

        LN = 9
        ZEROINGS = n_rows // P // 14
        DVE_SETUP = 10

        def hold(engine, passed):
            engine.sem_inc(passed, 1)

        block = ctx.enter_context(nc.Block())

        @block.sync
        def _(sp):
            for to, frm in (
                (select_st, select), (wm_a, wm_t[0:P, :]), (wm_b, wm_t[P:D, :]),
                (wu2_a, wu[D:D + P, :]), (wu2_b, wu[D + P:2 * D, :]),
                (ident_sb[:, :], ident), (sum_sb[:, :], sum_select), (lower_sb[:, :], lower),
                (trash_sb[:, :], trash), (wux_a[:, :], wu[0:P, :]), (wux_b[0:32, :], wu[P:D, :]),
                (wux_b[32:33, :], bu), (w3_sb[:, :], w3), (w4_sb[:, :, :], w4),
            ):
                sp.dma_start(to, frm).then_inc(consts_in, 16)
            sp.dma_start(w1_sb[:, :, :], w1).then_inc(consts_in, 16)
            sp.dma_start(w2_sb[:, :, :], w2).then_inc(consts_in, 16)

            def load_dst_e(g):
                if at_least(g, 2):
                    sp.wait_ge(x_gathered[g[1]], g[0] * 64)
                    sp.wait_ge(e_rests, number(g) * 2 - 2)
                sp.dma_start(dst_sb[g[1]][:, :], dst_idx[number(g), :, :]).then_inc(dst_e_in[g[1]], 16)
                sp.dma_start(e_sb[g[1]][:, :, :], edge_attr[number(g), :, :, :]).then_inc(dst_e_in[g[1]], 16)

            def load_src(g):
                if at_least(g, 2):
                    sp.wait_ge(idx_step, number(g) * 3 - 3)
                sp.dma_start(src_sb[g[1]][:, :], src_idx[number(g), :, :]).then_inc(src_in[g[1]], 16)
                sp.dma_start(row_sb[g[1]][:, :, :],
                             src_row[number(g), :, :].to_broadcast([P, GE])
                             .rearrange("p (s e) -> p s e", s=TILES)).then_inc(src_in[g[1]], 16)

            def slot(s):
                if not isinstance(s[0], int) or 0 <= number(s) + 3 < n_groups:
                    load_dst_e(shift(s, 3))
                if not isinstance(s[0], int) or 0 <= number(s) < n_groups:
                    load_src(s)

            run_slots(sp, slot, -3, n_groups, 2, (n_groups - 3) // 2 * 2)

            sp.wait_ge(scattered, 16 * TILES * n_groups)

            def load_nodes(c, parts):
                if at_least(c, 4, 4):
                    sp.wait_ge(ln_step, number(c, 4) * LN - 4 * LN + 1)
                b = c[1]
                rows = number(c, 4) * GE
                for to, frm in ((xn[b], x), (an[b], agg)):
                    sp.dma_start(to[0:parts, :],
                                 frm[bass.ds(rows, parts * TILES), :].rearrange("(p s) d -> p (s d)", s=TILES)
                                 ).then_inc(nodes_in[b], 16)

            def node_slot(c):
                parts = rest if isinstance(c[0], int) and number(c, 4) == full else P
                load_nodes(c, parts)

            run_slots(sp, node_slot, 0, n_out, 4, full // 4 * 4, 4)

        @block.gpsimd
        def _(pool):
            def gather(g, q):
                if q == 0:
                    pool.wait_ge(dst_e_in[g[1]], g[0] * 32 + 32)
                    if at_least(g, 2):
                        pool.wait_ge(x_spread, number(g) * 4 - 4)
                hold(pool, pool_passed)
                nc.gpsimd.indirect_dma_start(
                    xg[g[1]][:, q, :], None, x,
                    bass.IndirectOffsetOnAxis(dst_sb[g[1]][:, q:q + 1].bitcast(U32), 0)
                ).then_inc(x_gathered[g[1]], 16)

            def e_rest(g, step):
                pool.wait_ge(e_rounded, number(g) * 2 + step + 1)
                high, mid, low = (e3[g[1]][:, :, k, :] for k in range(3))
                if step == 0:
                    if at_least(g, 1):
                        pool.wait_ge(e_rests, number(g) * 2)
                    nc.gpsimd.tensor_tensor(e_low[:, :, :], e_sb[g[1]][:, :, :], high, ALU.subtract).then_inc(e_rests, 1)
                else:
                    pool.wait_ge(e_rests, number(g) * 2 + 1)
                    nc.gpsimd.tensor_tensor(low, e_low[:, :, :], mid, ALU.subtract).then_inc(e_rests, 1)

            def add_parts(g, step):
                if step == 0:
                    pool.wait_ge(multiplied, number(g) * NQ + NQ + 2)
                else:
                    pool.wait_ge(parts_added_pool, number(g) * 2 + 1)
                total = prod[g[1]][:, 16, :]
                nc.gpsimd.tensor_tensor(total, total, prod[g[1]][:, 18 + 2 * step, :],
                                        ALU.add).then_inc(parts_added_pool, 1)

            def mask_same(g):
                pool.wait_ge(same_done, number(g) + 1)
                if at_least(g, 2):
                    pool.wait_ge(summed_ready, number(g) - 1)
                nc.gpsimd.tensor_tensor(same_low[g[1]][:, :, :], same[g[1]][:, :, :],
                                        lower_sb[:, :].unsqueeze(1).to_broadcast([P, TILES, P]),
                                        ALU.mult).then_inc(same_low_done, 1)

            def scatter(g, q):
                if q == 0:
                    pool.wait_ge(summed_copied, number(g) + 1)
                    pool.wait_ge(idx_step, number(g) * 3 + 3)
                if at_least(g, 1) or q:
                    pool.wait_ge(scattered, number(g) * 64 + q * 16)
                else:
                    pool.wait_ge(table_zero, 16 * ZEROINGS)
                hold(pool, pool_passed)
                nc.gpsimd.indirect_dma_start(
                    agg, bass.IndirectOffsetOnAxis(row_idx[g[1]][:, q:q + 1].bitcast(U32), 0),
                    summed[g[1]][:, q // 2, q % 2 * D:(q % 2 + 1) * D], None, compute_op=ALU.add).then_inc(scattered, 16)

            pool.wait_ge(consts_in, 16 * 16)

            def slot(s):
                live = lambda d: not isinstance(s[0], int) or 0 <= number(s) + d < n_groups
                for q in range(TILES):
                    if live(-3):
                        scatter(shift(s, -3), q)
                    if live(2):
                        gather(shift(s, 2), q)
                    if q < 2 and live(-1):
                        add_parts(shift(s, -1), q)
                    if q == 2 and live(-1):
                        mask_same(shift(s, -1))
                    if q % 2 == 1 and live(2):
                        e_rest(shift(s, 2), q // 2)

            run_slots(pool, slot, -2, n_groups + 3, 4, (n_groups - 2) // 2 * 2)

            def node_slot(c):
                n = number(c, 4)
                parts = rest if isinstance(n, int) and n == full else P
                pool.wait_ge(normed, n + 1)
                hold(pool, pool_passed)
                pool.dma_start(out[bass.ds(n * GE, parts * TILES), :].rearrange("(p s) d -> p (s d)", s=TILES),
                               on[c[1]][0:parts, :]).then_inc(nodes_out[c[1]], 16)

            run_slots(pool, node_slot, 0, n_out, 4, full // 4 * 4, 4)
            for b in range(4):
                pool.wait_ge(nodes_out[b], 16 * ((n_out - b + 3) // 4))

        @block.scalar
        def _(act):
            act.wait_ge(consts_in, 16 * 16)
            half = 0.5 ** 0.5
            nc.scalar.mul(w1_sb[:, :, :], w1_sb[:, :, :], half / (64 * 8) ** 0.5).then_inc(scaled, 1)
            nc.scalar.mul(w2_sb[:, :, :], w2_sb[:, :, :], half / (3 * 32 * 8) ** 0.5).then_inc(scaled, 1)
            nc.scalar.mul(w3_sb[:, :], w3_sb[:, :], half / (64 * 8) ** 0.5).then_inc(scaled, 1)
            nc.scalar.mul(w4_sb[:, :, :], w4_sb[:, :, :], half / (32 * 8) ** 0.5).then_inc(scaled, 1)
            act.sem_inc(t_free, 2)

            def spread_x(g, k):
                if k == 0:
                    act.wait_ge(x_gathered[g[1]], g[0] * 64 + 64)
                    if at_least(g, 1):
                        act.wait_ge(t_ready, number(g) * USES - USES + 4)
                    frm = xg[g[1]][:, :, 0:NS].unsqueeze(2).to_broadcast([P, TILES, 2, NS])
                    to = spread[:, :, 0, :].rearrange("p q (r a) -> p q r a", r=2)
                else:
                    frm = xg[g[1]][:, :, NS + k - 1:D:3].unsqueeze(2).to_broadcast([P, TILES, 4, NV])
                    to = spread[:, :, k, :].rearrange("p q (r a) -> p q r a", r=4)
                nc.scalar.activation(to, frm, ACT.Copy).then_inc(x_spread, 1)

            def evacuate(g, k):
                if k == 0 and at_least(g, 2):
                    act.wait_ge(multiplied, number(g) * NQ - NQ + 2)
                act.wait_ge(t_ready, number(g) * USES + k + 1)
                bank = ps[:, T_BANK + (g[1] * USES + k) % 2, :]
                if k == 4:
                    to, frm = eT[g[1]][:, :], bank.bitcast(BF16)[0:3 * DE, 0:GE]
                else:
                    to, frm = XY[g[1]][:, k if k < 4 else k - 1, :], bank
                nc.scalar.activation(to, frm, ACT.Copy).then_inc(t_free, 1)

            def round_e(g, step):
                if step == 0:
                    act.wait_ge(dst_e_in[g[1]], g[0] * 32 + 32)
                    if at_least(g, 2):
                        act.wait_ge(t_ready, number(g) * USES - 2 * USES + 5)
                else:
                    act.wait_ge(e_rests, number(g) * 2 + 1)
                nc.scalar.activation(e3[g[1]][:, :, step, :], (e_low if step else e_sb[g[1]])[:, :, :],
                                     ACT.Copy).then_inc(e_rounded, 1)

            def zero_table(first, last):
                for k in range(first, last):
                    act.dma_start(agg.rearrange("(p k r) d -> p k (r d)", p=P, r=14)[:, k, :],
                                  zeros[:, :]).then_inc(table_zero, 16)

            def copy_S(g):
                act.wait_ge(S_ready, number(g) + 1)
                if at_least(g, 2):
                    act.wait_ge(msg_ready, number(g) - 1)
                nc.scalar.activation(S_sb[g[1]][:, :], ps[:, S_BANK, :], ACT.Copy).then_inc(S_copied, 1)

            def copy_V(g):
                act.wait_ge(V_ready, number(g) + 1)
                if at_least(g, 2):
                    act.wait_ge(msg_ready, number(g) - 1)
                nc.scalar.activation(V_sb[g[1]][0:96, :], ps[0:96, V_BANK, :], ACT.Copy).then_inc(V_copied, 1)

            def copy_msg(g):
                act.wait_ge(msg_ready, number(g) + 1)
                if at_least(g, 2):
                    act.wait_ge(summed_ready, number(g) - 1)
                nc.scalar.activation(msg[g[1]][:, :, :].rearrange("p (a b) d -> p a (b d)", a=2), msg_ps,
                                     ACT.Copy).then_inc(msg_copied, 1)

            def copy_summed(g):
                act.wait_ge(summed_ready, number(g) + 1)
                if at_least(g, 2):
                    act.wait_ge(scattered, number(g) * 64 - 64)
                nc.scalar.activation(summed[g[1]][:, :, :], sum_ps, ACT.Copy).then_inc(summed_copied, 1)

            def slot(s):
                live = lambda d: not isinstance(s[0], int) or 0 <= number(s) + d < n_groups
                if isinstance(s[0], int) and -1 <= number(s) < 3:
                    zero_table(ZEROINGS * (number(s) + 1) // 4, ZEROINGS * (number(s) + 2) // 4)
                if live(2):
                    round_e(shift(s, 2), 0)
                if live(1):
                    for k in range(4):
                        spread_x(shift(s, 1), k)
                if live(-2):
                    copy_msg(shift(s, -2))
                if live(1):
                    evacuate(shift(s, 1), 0)
                    evacuate(shift(s, 1), 1)
                if live(-2):
                    copy_summed(shift(s, -2))
                if live(2):
                    round_e(shift(s, 2), 1)
                if live(1):
                    for k in range(2, 5):
                        evacuate(shift(s, 1), k)
                if live(-1):
                    copy_S(shift(s, -1))
                if live(1):
                    evacuate(shift(s, 1), 5)
                    evacuate(shift(s, 1), 6)
                if live(-1):
                    copy_V(shift(s, -1))

            act.wait_ge(setup_done, 1)
            run_slots(act, slot, -2, n_groups + 2, 4, (n_groups - 2) // 2 * 2)

            def node_slot(c):
                n, b = number(c, 4), c[1]
                parts = rest if isinstance(n, int) and n == full else P
                if not isinstance(n, int) or n < n_out:
                    act.wait_ge(xT_ready, n + 1)
                    if at_least(c, 2, 4):
                        act.wait_ge(upd_ready, n - 1)
                    nc.scalar.activation(xTa[b % 2].rearrange("k (s p) -> k s p", s=TILES)[:, :, 0:parts],
                                         ps[:, 4 + b % 2, :].rearrange("k (s p) -> k s p", s=TILES)[:, :, 0:parts],
                                         ACT.Copy).then_inc(xT_copied, 1)
                    nc.scalar.activation(xTb[b % 2][0:32].rearrange("k (s p) -> k s p", s=TILES)[:, :, 0:parts],
                                         ps[0:32, 6 + b % 2, :].rearrange("k (s p) -> k s p", s=TILES)[:, :, 0:parts],
                                         ACT.Copy).then_inc(xT_copied, 1)
                if at_least(c, 1, 4) and not (isinstance(n, int) and n > n_out):
                    d = shift(c, -1, 4)
                    m, v = number(d, 4), d[1] % 2
                    parts = rest if isinstance(m, int) and m == full else P
                    act.wait_ge(ln_step, m * LN + LN)
                    if at_least(d, 2, 4):
                        act.wait_ge(rstd_step, m * 2 - 2)
                    nc.scalar.activation(std[v][0:parts], mv[v][0:parts, :, 1], ACT.Sqrt,
                                         bias=eps_sb[0:parts, :]).then_inc(std_done, 1)
                if at_least(c, 2, 4):
                    c = shift(c, -2, 4)
                    n, b = number(c, 4), c[1]
                    parts = rest if isinstance(n, int) and n == full else P
                    act.wait_ge(rstd_step, n * 2 + 2)
                    if at_least(c, 4, 4):
                        act.wait_ge(nodes_out[b], c[0] * 16)
                    for q in range(TILES):
                        last = nc.scalar.activation(on[b][0:parts, q * D:(q + 1) * D], yn[b][0:parts, q * D:(q + 1) * D],
                                                    ACT.Identity, bias=shift_n[b % 2][0:parts, q:q + 1],
                                                    scale=rstd[b % 2][0:parts, q:q + 1])
                    last.then_inc(normed, 1)

            run_slots(act, node_slot, 0, n_out + 2, 8, full // 4 * 4, 4)

        @block.vector
        def _(dve):
            nc.vector.memset(zeros[:, :], 0.0).then_inc(setup_done, 1)
            nc.vector.memset(ones_bf[:, :], 1.0).then_inc(setup_done, 1)
            nc.vector.memset(eps_sb[:, :], EPS).then_inc(setup_done, 1)
            for u in range(2):
                nc.vector.memset(V_sb[u][96:97, :], 1.0).then_inc(setup_done, 1)
            dve.wait_ge(consts_in, 16 * 16)
            nc.vector.tensor_copy(ident_bf[:, :], ident_sb[:, :]).then_inc(setup_done, 1)
            nc.vector.tensor_copy(select_sb[:, :], select_st).then_inc(setup_done, 1)
            nc.vector.scalar_tensor_tensor(wux_a[:, 0:P], ident_sb[:, :], 2.0, wux_a[:, 0:P],
                                           ALU.mult, ALU.add).then_inc(setup_done, 1)
            nc.vector.scalar_tensor_tensor(wux_b[0:32, P:D], ident_sb[0:32, 0:32], 2.0, wux_b[0:32, P:D],
                                           ALU.mult, ALU.add).then_inc(setup_done, 1)
            dve.wait_ge(wc_ready, 1)
            nc.vector.tensor_copy(wc_s[:, :], ps[:, M_BANK, 0:D]).then_inc(wc_copied, 1)
            nc.vector.tensor_copy(wc_v[:, :], ps[0:97, M_BANK + 1, 0:D]).then_inc(wc_copied, 1)
            dve.wait_ge(setup_done, DVE_SETUP - 1)
            nc.vector.memset(to_trash[:, :], 0.0).then_inc(setup_done, 1)
            dve.sem_inc(multiplied, 2)

            def multiply(g, q):
                if q == 0:
                    if at_least(g, 2):
                        dve.wait_ge(S_ready, number(g) - 1)
                        dve.wait_ge(V_ready, number(g) - 1)
                    dve.wait_ge(t_free, number(g) * USES + 6)
                if q == 6:
                    dve.wait_ge(t_free, number(g) * USES + 9)
                dve.wait_ge(e_ready, number(g) * NQ + q + 1)
                tiles = XY[g[1]]
                if q < 4:
                    count, first, frm = 1, q, tiles[:, 0:1, :]
                elif q < 6:
                    count, first, frm = 3, 4 + 3 * (q - 4), tiles[:, 1:4, :]
                else:
                    fours, i = divmod(q - 6, 3)
                    step = 4 + fours - (1 + i)
                    count, first, frm = 2, 10 + 2 * (q - 6), tiles[:, 1 + i:4 + fours + 1:step, :]
                edge = ps[:, E_BANK + q % 2, :].unsqueeze(1).to_broadcast([P, count, GE])
                nc.vector.tensor_tensor(prod[g[1]][:, first:first + count, :], frm, edge,
                                        ALU.mult).then_inc(multiplied, 1)

            def add_parts(g, step):
                if step == 0:
                    dve.wait_ge(multiplied, number(g) * NQ + 9 + 2)
                else:
                    dve.wait_ge(parts_added_dve, number(g) * 2 + 1)
                total = prod[g[1]][:, 10, :]
                nc.vector.tensor_tensor(total, total, prod[g[1]][:, 12 + 2 * step, :],
                                        ALU.add).then_inc(parts_added_dve, 1)

            def find_same(g):
                dve.wait_ge(src_in[g[1]], g[0] * 32 + 32)
                if at_least(g, 2):
                    dve.wait_ge(summed_ready, number(g) - 1)
                nc.vector.tensor_tensor(same[g[1]][:, :, :], row_sb[g[1]][:, :, :],
                                        src_sb[g[1]][:, :].unsqueeze(2).to_broadcast([P, TILES, P]),
                                        ALU.is_equal).then_inc(same_done, 1)

            def rows(g):
                n = number(g)
                if at_least(g, 1):
                    dve.wait_ge(idx_step, n * 3)
                dve.wait_ge(src_in[g[1]], g[0] * 32 + 32)
                nc.vector.tensor_tensor(to_trash[:, :], trash_sb[:, :], src_sb[g[1]][:, :],
                                        ALU.subtract).then_inc(idx_step, 1)
                dve.wait_ge(idx_step, n * 3 + 1)
                dve.wait_ge(summed_copied, n + 1)
                nc.vector.scalar_tensor_tensor(moved[:, :].rearrange("p (a b) -> p a b", a=2),
                                               summed[g[1]][:, :, 2 * D:2 * D + 2], 1.0,
                                               to_trash[:, :].rearrange("p (a b) -> p a b", a=2),
                                               ALU.min, ALU.mult).then_inc(idx_step, 1)
                dve.wait_ge(idx_step, n * 3 + 2)
                if at_least(g, 2):
                    dve.wait_ge(scattered, n * 64 - 64)
                nc.vector.tensor_tensor(row_idx[g[1]][:, :], moved[:, :], src_sb[g[1]][:, :],
                                        ALU.add).then_inc(idx_step, 1)

            dve.wait_ge(setup_done, DVE_SETUP)

            def slot(s):
                live = lambda d: not isinstance(s[0], int) or 0 <= number(s) + d < n_groups
                for q in range(NQ):
                    if live(0):
                        multiply(s, q)
                    if q in (9, 11) and live(0):
                        add_parts(s, q // 2 - 4)
                    if q == 0 and live(-1):
                        find_same(shift(s, -1))
                    if q == 7 and live(-2):
                        rows(shift(s, -2))

            run_slots(dve, slot, 0, n_groups + 2, 4, n_groups // 2 * 2)

            dve.wait_ge(scattered, 16 * TILES * n_groups)
            for b in range(2):
                nc.vector.memset(xTb[b][32:33, :], 1.0).then_inc(ones_set, 1)

            def node_slot(c):
                n, b = number(c, 4), c[1]
                parts = rest if isinstance(n, int) and n == full else P
                if not isinstance(n, int) or n < n_out:
                    dve.wait_ge(upd_ready, n + 1)
                    dve.wait_ge(nodes_in[b], c[0] * 32 + 32)
                    if at_least(c, 4, 4):
                        dve.wait_ge(normed, n - 3)
                    y, st, m = yn[b][0:parts], stats[b % 2][0:parts], mv[b % 2][0:parts]
                    nc.vector.tensor_tensor(y.rearrange("p (a e) -> p a e", a=2),
                                            ps[0:parts, 2 * (b % 2):2 * (b % 2) + 2, 0:2 * D],
                                            an[b][0:parts].rearrange("p (a e) -> p a e", a=2),
                                            ALU.add).then_inc(ln_step, 1)
                if at_least(c, 1, 4):
                    d = shift(c, -1, 4)
                    k, v = number(d, 4), d[1] % 2
                    some = rest if isinstance(k, int) and k == full else P
                    dve.wait_ge(std_done, k + 1)
                    if at_least(d, 2, 4):
                        dve.wait_ge(normed, k - 1)
                    nc.vector.reciprocal(rstd[v][0:some], std[v][0:some]).then_inc(rstd_step, 1)
                    dve.wait_ge(rstd_step, k * 2 + 1)
                    nc.vector.scalar_tensor_tensor(shift_n[v][0:some], mv[v][0:some, :, 0], -1.0,
                                                   rstd[v][0:some], ALU.mult, ALU.mult).then_inc(rstd_step, 1)
                if not isinstance(n, int) or n < n_out:
                    dve.wait_ge(ln_step, n * LN + 1)
                    for q in range(TILES):
                        nc.vector.bn_stats(st[:, q, :], y[:, q * D:(q + 1) * D]).then_inc(ln_step, 1)
                    if at_least(c, 2, 4):
                        dve.wait_ge(rstd_step, n * 2 - 2)
                    for q in range(TILES):
                        dve.wait_ge(ln_step, n * LN + 2 + q)
                        hold(dve, dve_passed)
                        nc.vector.bn_aggr(m[:, q, :], st[:, q, :]).then_inc(ln_step, 1)

            run_slots(dve, node_slot, 0, n_out + 1, 4, full // 4 * 4, 4)

        @block.tensor
        def _(pe):
            pe.wait_ge(consts_in, 16 * 16)
            nc.tensor.matmul(ps[:, M_BANK, 0:D], wm_a[:, 0:P], wu2_a, start=True, stop=False)
            nc.tensor.matmul(ps[:, M_BANK, 0:D], wm_b[:, 0:P], wu2_b, start=False, stop=True)
            nc.tensor.matmul(ps[0:97, M_BANK + 1, 0:D], wm_a[:, P:225], wu2_a, start=True, stop=False)
            nc.tensor.matmul(ps[0:97, M_BANK + 1, 0:D], wm_b[:, P:225], wu2_b, start=False,
                             stop=True).then_inc(wc_ready, 1)
            pe.wait_ge(wc_copied, 2)
            pe.wait_ge(setup_done, DVE_SETUP)
            pe.wait_ge(scaled, 4)

            def bank_free(g, k):
                pe.wait_ge(t_free, number(g) * USES + k + 1)

            def transpose_x(g, k):
                pe.wait_ge(x_spread, number(g) * 4 + k + 1)
                bank_free(g, k)
                for q in range(TILES):
                    last = nc.tensor.transpose(ps[:, T_BANK + (g[1] * USES + k) % 2, q * P:(q + 1) * P],
                                               spread[:, q, k, :], ident_sb[:, :])
                last.then_inc(t_ready, 1)

            def transpose_e(g):
                pe.wait_ge(e_rests, number(g) * 2 + 2)
                bank_free(g, 4)
                bank = ps[:, T_BANK + (g[1] * USES + 4) % 2, :].bitcast(BF16)
                for q in range(TILES):
                    last = nc.tensor.transpose(bank[0:3 * DE, q * P:(q + 1) * P],
                                               e3[g[1]][:, q, :, :].rearrange("p k c -> p (k c)"), ident_bf[:, :])
                last.then_inc(t_ready, 1)

            def times_w3(g, h):
                bank_free(g, 5 + h)
                nc.tensor.matmul(ps[:, T_BANK + (g[1] * USES + 5 + h) % 2, :], w3_sb[64 * h:64 * h + 64, :],
                                 XY[g[1]][64 * h:64 * h + 64, 0, :], start=True, stop=True).then_inc(t_ready, 1)

            def replicate(g, q):
                if q == 0:
                    pe.wait_ge(t_free, number(g) * USES + 7)
                pe.wait_ge(multiplied, number(g) * NQ + q + 1)
                nc.tensor.matmul(ps[:, E_BANK + q % 2, :], select_sb[:, q * P:(q + 1) * P], eT[g[1]][:, :],
                                 start=True, stop=True).then_inc(e_ready, 1)

            def contract_S(g, n):
                if n == 0:
                    pe.wait_ge(multiplied, number(g) * NQ + NQ + 2)
                    if at_least(g, 1):
                        pe.wait_ge(S_copied, number(g))
                if n == 2:
                    pe.wait_ge(parts_added_dve, number(g) * 2 + 2)
                    pe.wait_ge(parts_added_pool, number(g) * 2 + 2)
                for h in range(2):
                    k = 2 * n + h
                    tile, w = (k, w1_sb[:, k, :]) if k < 4 else (10 + 6 * (k - 4), w2_sb[:, k - 4, :])
                    last = nc.tensor.matmul(ps[64 * h:64 * h + 64, S_BANK, :], w, prod[g[1]][:, tile, :],
                                            start=n == 0, stop=n == 2)
                if n == 2:
                    last.then_inc(S_ready, 1)

            def contract_V(g, n):
                if n == 0:
                    pe.wait_ge(multiplied, number(g) * NQ + NQ + 2)
                    if at_least(g, 1):
                        pe.wait_ge(V_copied, number(g))
                for i in range(3):
                    tile, w = (4 + 3 * n + i, w4_sb[:, n, :]) if n < 2 else (11 + 2 * (3 * (n - 2) + i), sum_sb[:, :])
                    last = nc.tensor.matmul(ps[32 * i:32 * i + 32, V_BANK, :], w, prod[g[1]][:, tile, :],
                                            start=n == 0, stop=n == 3)
                if n == 3:
                    last.then_inc(V_ready, 1)

            def messages(g, first):
                pe.wait_ge(S_copied, number(g) + 1)
                pe.wait_ge(V_copied, number(g) + 1)
                if at_least(g, 1):
                    pe.wait_ge(summed_copied, number(g))
                for q in (first, first + 1):
                    to = msg_ps[:, q // 2, q % 2 * D:(q % 2 + 1) * D]
                    nc.tensor.matmul(to, S_sb[g[1]][:, q * P:(q + 1) * P], wc_s[:, :], start=True, stop=False)
                    last = nc.tensor.matmul(to, V_sb[g[1]][:, q * P:(q + 1) * P], wc_v[:, :], start=False, stop=True)
                if first:
                    last.then_inc(msg_ready, 1)

            def sum_same(g):
                pe.wait_ge(msg_copied, number(g) + 1)
                pe.wait_ge(same_done, number(g) + 1)
                pe.wait_ge(same_low_done, number(g) + 1)
                for q in range(TILES):
                    nc.tensor.matmul(msg_ps[:, q // 2, q % 2 * D:(q % 2 + 1) * D], same[g[1]][:, q, :],
                                     msg[g[1]][:, q, :], start=True, stop=True)
                for q in range(TILES):
                    last = nc.tensor.matmul(sum_ps[:, q // 2, 2 * D + q % 2:2 * D + q % 2 + 1], same_low[g[1]][:, q, :], ones_bf[:, :],
                                            start=True, stop=True)
                last.then_inc(summed_ready, 1)

            def slot(s):
                live = lambda d: not isinstance(s[0], int) or 0 <= number(s) + d < n_groups
                before, two_before, after = shift(s, -1), shift(s, -2), shift(s, 1)
                for q in range(NQ):
                    if live(0):
                        replicate(s, q)
                    if live(-2):
                        if q < 2:
                            messages(two_before, 2 * q)
                        if q == 4:
                            sum_same(two_before)
                    if live(1):
                        if q in (2, 5):
                            transpose_x(after, (q - 2) // 3 * 2)
                            transpose_x(after, (q - 2) // 3 * 2 + 1)
                        if q == 6:
                            transpose_e(after)
                        if q in (8, 9):
                            times_w3(after, q - 8)
                    if live(-1):
                        if q in (3, 5, 6):
                            contract_S(before, (3, 5, 6).index(q))
                        if q in (4, 7, 10, 11):
                            contract_V(before, (4, 7, 10, 11).index(q))

            run_slots(pe, slot, -1, n_groups + 2, 4, (n_groups - 1) // 2 * 2)

            pe.wait_ge(scattered, 16 * TILES * n_groups)
            pe.wait_ge(ones_set, 2)

            def node_slot(c):
                n, b = number(c, 4), c[1]
                if not isinstance(n, int) or n < n_out:
                    parts = rest if isinstance(n, int) and n == full else P
                    pe.wait_ge(nodes_in[b], c[0] * 32 + 32)
                    if at_least(c, 2, 4):
                        pe.wait_ge(xT_copied, n * 2 - 2)
                    for q in range(TILES):
                        row = xn[b][0:parts, q * D:(q + 1) * D]
                        nc.tensor.transpose(ps[:, 4 + b % 2, q * P:q * P + parts], row[:, 0:P],
                                            ident_sb[0:parts, 0:parts])
                        last = nc.tensor.transpose(ps[0:32, 6 + b % 2, q * P:q * P + parts], row[:, P:D],
                                                   ident_sb[0:parts, 0:parts])
                    last.then_inc(xT_ready, 1)
                if at_least(c, 1, 4):
                    c = shift(c, -1, 4)
                    n, b = number(c, 4), c[1]
                    parts = rest if isinstance(n, int) and n == full else P
                    pe.wait_ge(xT_copied, n * 2 + 2)
                    if at_least(c, 2, 4):
                        pe.wait_ge(ln_step, n * LN - 2 * LN + 1)
                    for q in range(TILES):
                        to = ps[0:parts, 2 * (b % 2) + q // 2, q % 2 * D:(q % 2 + 1) * D]
                        nc.tensor.matmul(to, xTa[b % 2][:, q * P:q * P + parts], wux_a[:, :], start=True, stop=False)
                        last = nc.tensor.matmul(to, xTb[b % 2][:, q * P:q * P + parts], wux_b[:, :],
                                                start=False, stop=True)
                    last.then_inc(upd_ready, 1)

            run_slots(pe, node_slot, 0, n_out + 1, 4, full // 4 * 4, 4)


def constants(n_nodes):
    import numpy as np

    r = np.arange(P)
    component = np.zeros((NQ, P), np.int64)
    for k in range(4):
        component[k] = 2 * k + r // 64
    for f in range(2):
        component[4 + f] = 4 * f + r // 32
        for i in range(3):
            component[6 + 3 * f + i] = 8 + 3 * (4 * f + r // 32) + i
    select = (np.arange(3 * DE)[:, None] % DE == component.reshape(1, -1)).astype(np.float32)
    sum_select = (r[:, None] % NV == np.arange(NV)[None, :]).astype(np.float32)
    lower = (r[:, None] < r[None, :]).astype(np.float32)
    trash = np.repeat((n_nodes + r)[:, None], TILES, 1).astype(np.float32)
    return {"ident": np.eye(P, dtype=np.float32), "select": select, "sum_select": sum_select,
            "lower": lower, "trash": trash}


def kernel(x, src, dst, edge_attr_32, node_vec1, L0_gnn_W1, L0_gnn_W2, L0_gnn_W3, L0_gnn_W4,
           L0_gnn_Wm, L0_gnn_bm, L0_gnn_Wu, L0_gnn_bu):
    import numpy as np
    import concourse.bacc as bacc
    from concourse.bass_utils import run_bass_kernel_spmd

    x, src, dst, e = (np.asarray(a) for a in (x, src, dst, edge_attr_32))
    W1, W2, W3, W4, Wm, bm, Wu, bu = (np.asarray(a) for a in (
        L0_gnn_W1, L0_gnn_W2, L0_gnn_W3, L0_gnn_W4, L0_gnn_Wm, L0_gnn_bm, L0_gnn_Wu, L0_gnn_bu))
    n_nodes, n_edges = x.shape[0], src.shape[0]
    groups = (n_edges + GE - 1) // GE
    pad = groups * GE - n_edges
    src_p = np.concatenate([src, np.full(pad, n_nodes, src.dtype)])
    dst_p = np.concatenate([dst, np.zeros(pad, dst.dtype)])
    e_p = np.concatenate([e, np.zeros((pad, DE), e.dtype)])
    vec = 64 + 3 * np.arange(NV)[None, :] + np.arange(3)[:, None]
    rows = np.concatenate([Wm[0:64], Wm[0:64], Wm[vec.reshape(-1)], bm[None, :]])
    arrays = {
        "x": x,
        "dst_idx": dst_p.reshape(groups, P, TILES),
        "src_idx": src_p.reshape(groups, P, TILES),
        "src_row": src_p.reshape(groups, P, TILES).transpose(0, 2, 1).reshape(groups, 1, GE),
        "edge_attr": e_p.reshape(groups, P, TILES, DE),
        "w1": W1.transpose(1, 0, 2).reshape(4, P, NS).transpose(1, 0, 2),
        "w2": W2.transpose(1, 0, 2).reshape(2, P, NS).transpose(1, 0, 2),
        "w3": W3.reshape(64, 2, P).transpose(1, 0, 2).reshape(P, P),
        "w4": W4.transpose(1, 0, 2).reshape(2, P, NV).transpose(1, 0, 2),
        "wm_t": rows.T,
        "wu": Wu,
        "bu": bu.reshape(1, D),
        **constants(n_nodes),
    }
    nc = bacc.Bacc("TRN2", target_bir_lowering=False, num_devices=1)
    feeds, aps = {}, []
    for name, a in arrays.items():
        a = np.ascontiguousarray(a)
        feeds[f"in_{name}"] = a
        aps.append(nc.dram_tensor(f"in_{name}", a.shape, mybir.dt.from_np(a.dtype), kind="ExternalInput").ap())
    out = nc.dram_tensor("out", [n_nodes, D], F32, kind="ExternalOutput").ap()
    build(nc, *aps, out)
    result = run_bass_kernel_spmd(nc, [feeds], core_ids=[0])
    return result.results[0]["out"]
```

```python
from contextlib import ExitStack

import concourse.bass as bass
from concourse import mybir

F32 = mybir.dt.float32
BF16 = mybir.dt.bfloat16
I32 = mybir.dt.int32
U32 = mybir.dt.uint32
ALU = mybir.AluOpType
ACT = mybir.ActivationFunctionType

P = 128
TILES = 4
M1 = 4
M2 = 8
SET_ROWS = 7
GE = P * TILES
D = 160
NS, NV, DE = 64, 32, 32
NQ = 12
NPROD = 22
USES = 7
EPS = 1e-5


def shift(group, by, m=M1):
    j, u = group
    return j + (u + by) // m, (u + by) % m


def number(group, m=M1):
    return group[0] * m + group[1]


def at_least(group, least, m=M1):
    return not isinstance(group[0], int) or number(group, m) >= least


def run_slots(engine, slot, first, last, loop_from, loop_to, m=M1):
    assert loop_from % m == 0 and loop_to % m == 0
    for s in range(first, loop_from):
        slot((s // m, s % m))
    with engine.Fori(loop_from // m, loop_to // m) as j:
        for u in range(m):
            slot((j, u))
    for s in range(loop_to, last):
        slot((s // m, s % m))


def build(nc, x, x_t, dst_idx, src_idx, src_row, edge_attr, w1, w2, w3, w4, wm_t, wu, bu, ident, select,
          sum_select, lower, trash, out):
    n_nodes = x.shape[0]
    n_groups = dst_idx.shape[0]
    n_rows = (n_nodes + 2 * P - 1) // P * P
    full = n_nodes // GE
    rest = (n_nodes - full * GE) // TILES
    n_out = full + (rest > 0)
    assert rest * TILES + full * GE == n_nodes

    agg = nc.dram_tensor("agg", [n_rows, D], F32, kind="Internal").ap()

    with ExitStack() as ctx:
        def sb(name, shape, dt=F32):
            return ctx.enter_context(nc.sbuf_tensor(name, shape, dt))

        def two(name, shape, dt=F32):
            return [sb(f"{name}{u}", shape, dt) for u in range(2)]

        def sem(name):
            return ctx.enter_context(nc.semaphore(name))

        ident_sb = sb("ident_sb", [P, P])
        ident_bf = sb("ident_bf", [P, P], BF16)
        select_sb = sb("select_sb", [3 * DE, NQ * P], BF16)
        sum_sb = sb("sum_sb", [P, NV])
        lower_sb = sb("lower_sb", [P, P])
        trash_sb = sb("trash_sb", [P, TILES])
        ones_bf = sb("ones_bf", [P, 1], BF16)
        w1_sb = sb("w1_sb", [P, 4, NS])
        w2_sb = sb("w2_sb", [P, 2, NS])
        w3_sb = sb("w3_sb", [P, P])
        w4_sb = sb("w4_sb", [P, 2, NV])
        wc_s = sb("wc_s", [P, D])
        wc_v = sb("wc_v", [97, D])
        wux_a = sb("wux_a", [P, D])
        wux_b = sb("wux_b", [P, TILES, D])
        start_rows = sb("start_rows", [P, SET_ROWS * D])
        dst_sb = [sb(f"dst_sb{u}", [P, TILES], I32) for u in range(M1)]
        src_sb = [sb(f"src_sb{u}", [P, TILES], I32) for u in range(M1)]
        row_sb = [sb(f"row_sb{u}", [P, TILES, P], I32) for u in range(M1)]
        e_sb = [sb(f"e_sb{u}", [P, TILES, DE]) for u in range(M1)]
        e_low = sb("e_low", [P, TILES, DE])
        e3 = two("e3", [P, TILES, 3, DE], BF16)
        xg = two("xg", [P, TILES, D])
        spread = sb("spread", [P, TILES, 4, P])
        eT = two("eT", [3 * DE, GE], BF16)
        XY = two("XY", [P, 6, GE])
        prod = two("prod", [P, NPROD, GE])
        S_sb = two("S_sb", [P, GE])
        V_sb = two("V_sb", [97, GE])
        same = two("same", [P, TILES, P])
        same_low = two("same_low", [P, TILES, P], BF16)
        msg = two("msg", [P, TILES, D])
        summed = [sb(f"summed{u}", [P, 2, 2 * D + 2]) for u in range(M1)]
        to_trash = sb("to_trash", [P, TILES])
        moved = sb("moved", [P, TILES])
        row_idx = [sb(f"row_idx{u}", [P, TILES], I32) for u in range(M1)]
        stage = prod[0][:, :, :].rearrange("p n e -> p (n e)")
        wm_a, wm_b = stage[:, 0:225], stage[0:32, 225:450]
        wu2_a, wu2_b = stage[:, 450:610], stage[0:32, 610:770]
        wux_st = stage[:, 770:930]
        select_st = stage[0:3 * DE, 1024:1024 + NQ * P]
        nodes = prod[0][:, :, :].rearrange("p n e -> p (n e)")
        nodes2 = prod[1][:, :, :].rearrange("p n e -> p (n e)")
        an = [nodes[:, b * 640:(b + 1) * 640] for b in range(4)]
        yn = [nodes[:, (4 + b) * 640:(5 + b) * 640] for b in range(4)]
        on = [nodes[:, (8 + b) * 640:(9 + b) * 640] for b in range(4)]
        xT = [nodes2[:, b * 640:(b + 1) * 640] for b in range(M2)]
        stats = two("stats", [P, TILES, 6])
        mv = two("mv", [P, TILES, 2])
        eps_sb = sb("eps_sb", [P, 1])
        std = two("std", [P, TILES])
        rstd = two("rstd", [P, TILES])
        shift_n = two("shift_n", [P, TILES])

        ps = ctx.enter_context(nc.psum_tensor("ps", [P, 8, 512], F32))
        M_BANK, S_BANK, V_BANK, T_BANK, E_BANK = 0, 2, 3, 4, 6
        msg_ps = ps[:, M_BANK:M_BANK + 2, 0:2 * D]
        sum_ps = ps[:, M_BANK:M_BANK + 2, 0:2 * D + 2]

        consts_in = sem("consts_in")
        start_rows_in = sem("start_rows_in")
        table_set = [sem(f"table_set{u}") for u in range(3)]
        dst_e_in = [sem(f"dst_e_in{u}") for u in range(M1)]
        src_in = [sem(f"src_in{u}") for u in range(M1)]
        x_gathered = [sem(f"x_gathered{u}") for u in range(M1)]
        scattered = sem("scattered")
        xT_in = [sem(f"xT_in{b}") for b in range(M2)]
        agg_in = [sem(f"agg_in{b}") for b in range(M2)]
        nodes_out = [sem(f"nodes_out{b}") for b in range(M2)]
        e_rests = sem("e_rests")
        parts_added_pool = sem("parts_added_pool")
        same_low_done = sem("same_low_done")
        pool_passed = sem("pool_passed")
        wc_ready = sem("wc_ready")
        t_ready = sem("t_ready")
        e_ready = sem("e_ready")
        S_ready = sem("S_ready")
        V_ready = sem("V_ready")
        msg_ready = sem("msg_ready")
        summed_ready = sem("summed_ready")
        upd_ready = sem("upd_ready")
        x_spread = sem("x_spread")
        e_rounded = sem("e_rounded")
        scaled = sem("scaled")
        t_free = sem("t_free")
        S_copied = sem("S_copied")
        V_copied = sem("V_copied")
        msg_copied = sem("msg_copied")
        summed_copied = sem("summed_copied")
        std_done = sem("std_done")
        normed = sem("normed")
        setup_done = sem("setup_done")
        wc_copied = sem("wc_copied")
        multiplied = sem("multiplied")
        parts_added_dve = sem("parts_added_dve")
        same_done = sem("same_done")
        idx_step = sem("idx_step")
        ln_step = sem("ln_step")
        dve_passed = sem("dve_passed")
        rstd_step = sem("rstd_step")

        LN = 9
        CONSTS = 18
        STEADY = 20
        AHEAD = M2 - 1
        PIECES = n_rows // P // SET_ROWS
        DVE_SETUP = 14

        def hold(engine, passed):
            engine.sem_inc(passed, 1)

        block = ctx.enter_context(nc.Block())

        @block.sync
        def _(sp):
            def load_dst_e(g):
                if at_least(g, 4):
                    sp.wait_ge(x_gathered[g[1]], g[0] * 64)
                    sp.wait_ge(e_rests, number(g) * 2 - 6)
                sp.dma_start(dst_sb[g[1]][:, :], dst_idx[number(g), :, :]).then_inc(dst_e_in[g[1]], 16)
                sp.dma_start(e_sb[g[1]][:, :, :], edge_attr[number(g), :, :, :]).then_inc(dst_e_in[g[1]], 16)

            def start_table(k):
                if k >= 3:
                    sp.wait_ge(table_set[k % 3], 16 * (k // 3))
                sp.dma_start(agg.rearrange("(p k r) d -> p k (r d)", p=P, r=SET_ROWS)[:, k, :],
                             start_rows[:, :]).then_inc(table_set[k % 3], 16)

            def load_src(g):
                if at_least(g, 4):
                    sp.wait_ge(idx_step, number(g) * 3 - 9)
                sp.dma_start(src_sb[g[1]][:, :], src_idx[number(g), :, :]).then_inc(src_in[g[1]], 16)
                sp.dma_start(row_sb[g[1]][:, :, :],
                             src_row[number(g), :, :].to_broadcast([P, GE])
                             .rearrange("p (s e) -> p s e", s=TILES)).then_inc(src_in[g[1]], 16)

            def slot(s):
                if not isinstance(s[0], int) or 0 <= number(s) + 5 < n_groups:
                    load_dst_e(shift(s, 5))
                if not isinstance(s[0], int) or 0 <= number(s) < n_groups:
                    load_src(s)
                if isinstance(s[0], int) and number(s) < 5:
                    for k in range(PIECES * (number(s) + 1) // 6, PIECES * (number(s) + 2) // 6):
                        start_table(k)

            load_dst_e((0, 0))
            load_dst_e((0, 1))
            sp.dma_start(start_rows[:, :].rearrange("p (r d) -> p r d", r=SET_ROWS),
                         bu.unsqueeze(0).to_broadcast([P, SET_ROWS, D])).then_inc(start_rows_in, 16)
            for to, frm in (
                (select_st, select), (wm_a, wm_t[0:P, :]), (wm_b, wm_t[P:D, :]),
                (wu2_a, wu[D:D + P, :]), (wu2_b, wu[D + P:2 * D, :]),
                (ident_sb[:, :], ident), (sum_sb[:, :], sum_select), (lower_sb[:, :], lower),
                (trash_sb[:, :], trash), (wux_a[:, :], wu[0:P, :]),
                *((wux_st[32 * q:32 * q + 32, :], wu[P:D, :]) for q in range(TILES)), (w3_sb[:, :], w3), (w4_sb[:, :, :], w4),
            ):
                sp.dma_start(to, frm).then_inc(consts_in, 16)
            sp.dma_start(w1_sb[:, :, :], w1).then_inc(consts_in, 16)
            sp.dma_start(w2_sb[:, :, :], w2).then_inc(consts_in, 16)
            load_dst_e((0, 2))
            load_dst_e((0, 3))
            sp.wait_ge(start_rows_in, 16)
            run_slots(sp, slot, -1, n_groups, 8, (n_groups - 5) // M1 * M1)

            def load_xT(c):
                if at_least(c, M2, M2):
                    sp.wait_ge(upd_ready, number(c, M2) - M2 + 1)
                sp.dma_start(xT[c[1]], x_t[number(c, M2), :, :]).then_inc(xT_in[c[1]], 16)

            def load_agg(c):
                if at_least(c, 4, M2):
                    sp.wait_ge(ln_step, number(c, M2) * LN - 4 * LN + 1)
                parts = rest if isinstance(c[0], int) and number(c, M2) == full else P
                sp.dma_start(an[c[1] % 4][0:parts, :],
                             agg[bass.ds(number(c, M2) * GE, parts * TILES), :].rearrange("(p s) d -> p (s d)", s=TILES)
                             ).then_inc(agg_in[c[1]], 16)

            sp.wait_ge(S_ready, n_groups)
            sp.wait_ge(V_ready, n_groups)
            for b in range(AHEAD):
                load_xT((0, b))
            sp.wait_ge(scattered, 16 * TILES * n_groups)

            def node_slot(c):
                load_agg(c)
                if not isinstance(c[0], int) or number(c, M2) + AHEAD < n_out:
                    load_xT(shift(c, AHEAD, M2))

            run_slots(sp, node_slot, 0, n_out, M2, (full - AHEAD) // M2 * M2, M2)

        @block.gpsimd
        def _(pool):
            def gather(g, q):
                if q == 0:
                    pool.wait_ge(dst_e_in[g[1]], g[0] * 32 + 32)
                    if at_least(g, 2):
                        pool.wait_ge(x_spread, number(g) * 4 - 4)
                hold(pool, pool_passed)
                nc.gpsimd.indirect_dma_start(
                    xg[g[1] % 2][:, q, :], None, x,
                    bass.IndirectOffsetOnAxis(dst_sb[g[1]][:, q:q + 1].bitcast(U32), 0)
                ).then_inc(x_gathered[g[1]], 16)

            def e_rest(g, step):
                pool.wait_ge(e_rounded, number(g) * 2 + step + 1)
                high, mid, low = (e3[g[1] % 2][:, :, k, :] for k in range(3))
                if step == 0:
                    if at_least(g, 1):
                        pool.wait_ge(e_rests, number(g) * 2)
                    nc.gpsimd.tensor_tensor(e_low[:, :, :], e_sb[g[1]][:, :, :], high, ALU.subtract).then_inc(e_rests, 1)
                else:
                    pool.wait_ge(e_rests, number(g) * 2 + 1)
                    nc.gpsimd.tensor_tensor(low, e_low[:, :, :], mid, ALU.subtract).then_inc(e_rests, 1)

            def add_parts(g, step):
                if step == 0:
                    pool.wait_ge(multiplied, number(g) * NQ + NQ + 2)
                else:
                    pool.wait_ge(parts_added_pool, number(g) * 2 + 1)
                total = prod[g[1] % 2][:, 16, :]
                nc.gpsimd.tensor_tensor(total, total, prod[g[1] % 2][:, 18 + 2 * step, :],
                                        ALU.add).then_inc(parts_added_pool, 1)

            def mask_same(g):
                if not at_least(g, 1):
                    pool.wait_ge(consts_in, 16 * CONSTS)
                pool.wait_ge(same_done, number(g) + 1)
                if at_least(g, 2):
                    pool.wait_ge(summed_ready, number(g) - 1)
                nc.gpsimd.tensor_tensor(same_low[g[1] % 2][:, :, :], same[g[1] % 2][:, :, :],
                                        lower_sb[:, :].unsqueeze(1).to_broadcast([P, TILES, P]),
                                        ALU.mult).then_inc(same_low_done, 1)

            def scatter(g, q):
                if q == 0:
                    pool.wait_ge(summed_copied, number(g) + 1)
                    pool.wait_ge(idx_step, number(g) * 3 + 3)
                if at_least(g, 1) or q:
                    pool.wait_ge(scattered, number(g) * 64 + q * 16)
                else:
                    for u in range(3):
                        pool.wait_ge(table_set[u], 16 * ((PIECES - u + 2) // 3))
                hold(pool, pool_passed)
                nc.gpsimd.indirect_dma_start(
                    agg, bass.IndirectOffsetOnAxis(row_idx[g[1]][:, q:q + 1].bitcast(U32), 0),
                    summed[g[1]][:, q // 2, q % 2 * D:(q % 2 + 1) * D], None, compute_op=ALU.add).then_inc(scattered, 16)

            def first_tile(n):
                return max(0, min(TILES * (n - 3), 19 * (n - 5) // 4 - 2))

            assert first_tile(STEADY) == TILES * (STEADY - 3)

            def slot(s):
                live = lambda d: not isinstance(s[0], int) or 0 <= number(s) + d < n_groups
                if isinstance(s[0], int) and number(s) < STEADY:
                    tiles = [((t // TILES // M1, t // TILES % M1), t % TILES)
                             for t in range(first_tile(number(s)), first_tile(number(s) + 1))]
                    split = 0 if number(s) == 5 else TILES
                else:
                    split = TILES
                    tiles = [(shift(s, -3), q) for q in range(TILES)] if live(-3) else []
                for q in range(TILES):
                    for tile in tiles[:split][q:q + 1]:
                        scatter(*tile)
                    if live(2):
                        gather(shift(s, 2), q)
                    if q < 2 and live(-1):
                        add_parts(shift(s, -1), q)
                    if q == 2 and live(-1):
                        mask_same(shift(s, -1))
                    if q % 2 == 1 and live(2):
                        e_rest(shift(s, 2), q // 2)
                for tile in tiles[split:]:
                    scatter(*tile)

            run_slots(pool, slot, -2, n_groups + 3, STEADY, (n_groups - 2) // M1 * M1)

            def node_slot(c):
                n = number(c, M2)
                parts = rest if isinstance(n, int) and n == full else P
                pool.wait_ge(normed, n + 1)
                hold(pool, pool_passed)
                pool.dma_start(out[bass.ds(n * GE, parts * TILES), :].rearrange("(p s) d -> p (s d)", s=TILES),
                               on[c[1] % 4][0:parts, :]).then_inc(nodes_out[c[1]], 16)

            run_slots(pool, node_slot, 0, n_out, M2, full // M2 * M2, M2)
            for b in range(M2):
                pool.wait_ge(nodes_out[b], 16 * ((n_out - b + M2 - 1) // M2))

        @block.scalar
        def _(act):
            act.wait_ge(consts_in, 16 * CONSTS)
            half = 0.5 ** 0.5
            nc.scalar.mul(w1_sb[:, :, :], w1_sb[:, :, :], half / (64 * 8) ** 0.5).then_inc(scaled, 1)
            nc.scalar.mul(w2_sb[:, :, :], w2_sb[:, :, :], half / (3 * 32 * 8) ** 0.5).then_inc(scaled, 1)
            nc.scalar.mul(w3_sb[:, :], w3_sb[:, :], half / (64 * 8) ** 0.5).then_inc(scaled, 1)
            nc.scalar.mul(w4_sb[:, :, :], w4_sb[:, :, :], half / (32 * 8) ** 0.5).then_inc(scaled, 1)
            act.sem_inc(t_free, 2)

            def spread_x(g, k):
                if k == 0:
                    act.wait_ge(x_gathered[g[1]], g[0] * 64 + 64)
                    if at_least(g, 1):
                        act.wait_ge(t_ready, number(g) * USES - USES + 5)
                    frm = xg[g[1] % 2][:, :, 0:NS].unsqueeze(2).to_broadcast([P, TILES, 2, NS])
                    to = spread[:, :, 0, :].rearrange("p q (r a) -> p q r a", r=2)
                else:
                    frm = xg[g[1] % 2][:, :, NS + k - 1:D:3].unsqueeze(2).to_broadcast([P, TILES, 4, NV])
                    to = spread[:, :, k, :].rearrange("p q (r a) -> p q r a", r=4)
                nc.scalar.activation(to, frm, ACT.Copy).then_inc(x_spread, 1)

            def evacuate(g, k):
                if k == 0 and at_least(g, 2):
                    act.wait_ge(multiplied, number(g) * NQ - NQ + 2)
                act.wait_ge(t_ready, number(g) * USES + k + 1)
                bank = ps[:, T_BANK + (g[1] * USES + k) % 2, :]
                if k == 0:
                    to, frm = eT[g[1] % 2][:, :], bank.bitcast(BF16)[0:3 * DE, 0:GE]
                else:
                    to, frm = XY[g[1] % 2][:, k - 1, :], bank
                nc.scalar.activation(to, frm, ACT.Copy).then_inc(t_free, 1)

            def round_e(g, step):
                if step == 0:
                    act.wait_ge(dst_e_in[g[1]], g[0] * 32 + 32)
                    if at_least(g, 2):
                        act.wait_ge(t_ready, number(g) * USES - 2 * USES + 1)
                else:
                    act.wait_ge(e_rests, number(g) * 2 + 1)
                nc.scalar.activation(e3[g[1] % 2][:, :, step, :], (e_low if step else e_sb[g[1]])[:, :, :],
                                     ACT.Copy).then_inc(e_rounded, 1)

            def copy_S(g):
                act.wait_ge(S_ready, number(g) + 1)
                if at_least(g, 2):
                    act.wait_ge(msg_ready, number(g) - 1)
                nc.scalar.activation(S_sb[g[1] % 2][:, :], ps[:, S_BANK, :], ACT.Copy).then_inc(S_copied, 1)

            def copy_V(g):
                act.wait_ge(V_ready, number(g) + 1)
                if at_least(g, 2):
                    act.wait_ge(msg_ready, number(g) - 1)
                nc.scalar.activation(V_sb[g[1] % 2][0:96, :], ps[0:96, V_BANK, :], ACT.Copy).then_inc(V_copied, 1)

            def copy_msg(g):
                act.wait_ge(msg_ready, number(g) + 1)
                if at_least(g, 2):
                    act.wait_ge(summed_ready, number(g) - 1)
                nc.scalar.activation(msg[g[1] % 2][:, :, :].rearrange("p (a b) d -> p a (b d)", a=2), msg_ps,
                                     ACT.Copy).then_inc(msg_copied, 1)

            def copy_summed(g):
                act.wait_ge(summed_ready, number(g) + 1)
                if at_least(g, 4):
                    act.wait_ge(scattered, number(g) * 64 - 192)
                nc.scalar.activation(summed[g[1]][:, :, :], sum_ps, ACT.Copy).then_inc(summed_copied, 1)

            def slot(s):
                live = lambda d: not isinstance(s[0], int) or 0 <= number(s) + d < n_groups
                if live(0):
                    for k in range(4, 7):
                        evacuate(s, k)
                if live(2):
                    round_e(shift(s, 2), 0)
                if live(1):
                    evacuate(shift(s, 1), 0)
                    for k in range(2):
                        spread_x(shift(s, 1), k)
                if live(-2):
                    copy_msg(shift(s, -2))
                if live(1):
                    for k in range(2, 4):
                        spread_x(shift(s, 1), k)
                if live(-2):
                    copy_summed(shift(s, -2))
                if live(2):
                    round_e(shift(s, 2), 1)
                if live(1):
                    evacuate(shift(s, 1), 1)
                if live(-1):
                    copy_V(shift(s, -1))
                if live(1):
                    evacuate(shift(s, 1), 2)
                    evacuate(shift(s, 1), 3)
                if live(-1):
                    copy_S(shift(s, -1))

            run_slots(act, slot, -2, n_groups + 2, 8, (n_groups - 2) // M1 * M1)

            def node_slot(c):
                n, v = number(c, M2), c[1] % 2
                if at_least(c, 1, M2):
                    d = shift(c, -1, M2)
                    m, b = number(d, M2), d[1] % 4
                    parts = rest if isinstance(m, int) and m == full else P
                    act.wait_ge(rstd_step, m * 2 + 2)
                    if at_least(d, 4, M2):
                        stored = shift(d, -4, M2)
                        act.wait_ge(nodes_out[stored[1]], stored[0] * 16 + 16)
                    for q in range(TILES):
                        last = nc.scalar.activation(on[b][0:parts, q * D:(q + 1) * D], yn[b][0:parts, q * D:(q + 1) * D],
                                                    ACT.Identity, bias=shift_n[b % 2][0:parts, q:q + 1],
                                                    scale=rstd[b % 2][0:parts, q:q + 1])
                    last.then_inc(normed, 1)
                if not isinstance(n, int) or n < n_out:
                    parts = rest if isinstance(n, int) and n == full else P
                    act.wait_ge(ln_step, n * LN + LN)
                    if at_least(c, 2, M2):
                        act.wait_ge(rstd_step, n * 2 - 2)
                    nc.scalar.activation(std[v][0:parts], mv[v][0:parts, :, 1], ACT.Sqrt,
                                         bias=eps_sb[0:parts, :]).then_inc(std_done, 1)

            run_slots(act, node_slot, 0, n_out + 1, M2, full // M2 * M2, M2)

        @block.vector
        def _(dve):
            nc.vector.memset(ones_bf[:, :], 1.0).then_inc(setup_done, 1)
            nc.vector.memset(eps_sb[:, :], EPS).then_inc(setup_done, 1)
            for u in range(2):
                nc.vector.memset(V_sb[u][96:97, :], 1.0).then_inc(setup_done, 1)
            dve.wait_ge(consts_in, 16 * CONSTS)
            nc.vector.tensor_copy(ident_bf[:, :], ident_sb[:, :]).then_inc(setup_done, 1)
            nc.vector.tensor_copy(select_sb[:, :], select_st).then_inc(setup_done, 1)
            nc.vector.scalar_tensor_tensor(wux_a[:, 0:P], ident_sb[:, :], 2.0, wux_a[:, 0:P],
                                           ALU.mult, ALU.add).then_inc(setup_done, 1)
            nc.vector.memset(wux_b[:, :, :], 0.0).then_inc(setup_done, 1)
            nc.vector.scalar_tensor_tensor(wux_st[:, P:D], sum_sb[:, :], 2.0, wux_st[:, P:D],
                                           ALU.mult, ALU.add).then_inc(setup_done, 1)
            dve.wait_ge(setup_done, 9)
            for q in range(TILES):
                rows = slice(32 * q, 32 * q + 32)
                nc.vector.tensor_copy(wux_b[rows, q, :], wux_st[rows, :]).then_inc(setup_done, 1)
            dve.wait_ge(wc_ready, 1)
            nc.vector.tensor_copy(wc_s[:, :], ps[:, M_BANK, 0:D]).then_inc(wc_copied, 1)
            nc.vector.tensor_copy(wc_v[:, :], ps[0:97, M_BANK + 1, 0:D]).then_inc(wc_copied, 1)
            dve.wait_ge(setup_done, DVE_SETUP - 1)
            nc.vector.memset(to_trash[:, :], 0.0).then_inc(setup_done, 1)
            dve.sem_inc(multiplied, 2)

            def multiply(g, q):
                if q == 0:
                    if at_least(g, 2):
                        dve.wait_ge(S_ready, number(g) - 1)
                        dve.wait_ge(V_ready, number(g) - 1)
                    dve.wait_ge(t_free, number(g) * USES + 4)
                if q == 4:
                    dve.wait_ge(t_free, number(g) * USES + 7)
                if q == 6:
                    dve.wait_ge(t_free, number(g) * USES + 9)
                dve.wait_ge(e_ready, number(g) * NQ + q + 1)
                tiles = XY[g[1] % 2]
                if q < 4:
                    count, first, frm = 1, q, tiles[:, 0:1, :]
                elif q < 6:
                    count, first, frm = 3, 4 + 3 * (q - 4), tiles[:, 1:4, :]
                else:
                    fours, i = divmod(q - 6, 3)
                    step = 4 + fours - (1 + i)
                    count, first, frm = 2, 10 + 2 * (q - 6), tiles[:, 1 + i:4 + fours + 1:step, :]
                edge = ps[:, E_BANK + q % 2, :].unsqueeze(1).to_broadcast([P, count, GE])
                nc.vector.tensor_tensor(prod[g[1] % 2][:, first:first + count, :], frm, edge,
                                        ALU.mult).then_inc(multiplied, 1)

            def add_parts(g, step):
                if step == 0:
                    dve.wait_ge(multiplied, number(g) * NQ + 9 + 2)
                else:
                    dve.wait_ge(parts_added_dve, number(g) * 2 + 1)
                total = prod[g[1] % 2][:, 10, :]
                nc.vector.tensor_tensor(total, total, prod[g[1] % 2][:, 12 + 2 * step, :],
                                        ALU.add).then_inc(parts_added_dve, 1)

            def find_same(g):
                dve.wait_ge(src_in[g[1]], g[0] * 32 + 32)
                if at_least(g, 2):
                    dve.wait_ge(summed_ready, number(g) - 1)
                nc.vector.tensor_tensor(same[g[1] % 2][:, :, :], row_sb[g[1]][:, :, :],
                                        src_sb[g[1]][:, :].unsqueeze(2).to_broadcast([P, TILES, P]),
                                        ALU.is_equal).then_inc(same_done, 1)

            def rows(g, step):
                n = number(g)
                if step == 1:
                    dve.wait_ge(idx_step, n * 3 + 1)
                    dve.wait_ge(summed_copied, n + 1)
                    nc.vector.scalar_tensor_tensor(moved[:, :].rearrange("p (a b) -> p a b", a=2),
                                                   summed[g[1]][:, :, 2 * D:2 * D + 2], 1.0,
                                                   to_trash[:, :].rearrange("p (a b) -> p a b", a=2),
                                                   ALU.min, ALU.mult).then_inc(idx_step, 1)
                    return
                if step == 2:
                    dve.wait_ge(idx_step, n * 3 + 2)
                    if at_least(g, 4):
                        dve.wait_ge(scattered, n * 64 - 192)
                    nc.vector.tensor_tensor(row_idx[g[1]][:, :], moved[:, :], src_sb[g[1]][:, :],
                                            ALU.add).then_inc(idx_step, 1)
                    return
                if at_least(g, 1):
                    dve.wait_ge(idx_step, n * 3)
                dve.wait_ge(src_in[g[1]], g[0] * 32 + 32)
                nc.vector.tensor_tensor(to_trash[:, :], trash_sb[:, :], src_sb[g[1]][:, :],
                                        ALU.subtract).then_inc(idx_step, 1)

            dve.wait_ge(setup_done, DVE_SETUP)

            def slot(s):
                live = lambda d: not isinstance(s[0], int) or 0 <= number(s) + d < n_groups
                for q in range(NQ):
                    if q in (1, 6) and live(-1):
                        add_parts(shift(s, -1), q // 6)
                    if q == 3 and live(-1):
                        find_same(shift(s, -1))
                    if q in (3, 9, 11) and live(-2):
                        rows(shift(s, -2), (3, 9, 11).index(q))
                    if live(0):
                        multiply(s, q)

            run_slots(dve, slot, 0, n_groups + 2, 8, n_groups // M1 * M1)

            def node_slot(c):
                n, b, v = number(c, M2), c[1] % 4, c[1] % 2
                parts = rest if isinstance(n, int) and n == full else P
                y, st, m = yn[b][0:parts], stats[v][0:parts], mv[v][0:parts]
                if not isinstance(n, int) or n < n_out:
                    dve.wait_ge(upd_ready, n + 1)
                    dve.wait_ge(agg_in[c[1]], c[0] * 16 + 16)
                    if at_least(c, 4, M2):
                        dve.wait_ge(normed, n - 3)
                    nc.vector.tensor_tensor(y.rearrange("p (a e) -> p a e", a=2),
                                            ps[0:parts, 2 * b:2 * b + 2, 0:2 * D],
                                            an[b][0:parts].rearrange("p (a e) -> p a e", a=2),
                                            ALU.add).then_inc(ln_step, 1)
                if at_least(c, 1, M2):
                    d = shift(c, -1, M2)
                    k, w = number(d, M2), d[1] % 2
                    some = rest if isinstance(k, int) and k == full else P
                    dve.wait_ge(std_done, k + 1)
                    if at_least(d, 2, M2):
                        dve.wait_ge(normed, k - 1)
                    nc.vector.reciprocal(rstd[w][0:some], std[w][0:some]).then_inc(rstd_step, 1)
                    dve.wait_ge(rstd_step, k * 2 + 1)
                    nc.vector.scalar_tensor_tensor(shift_n[w][0:some], mv[w][0:some, :, 0], -1.0,
                                                   rstd[w][0:some], ALU.mult, ALU.mult).then_inc(rstd_step, 1)
                if not isinstance(n, int) or n < n_out:
                    dve.wait_ge(ln_step, n * LN + 1)
                    for q in range(TILES):
                        nc.vector.bn_stats(st[:, q, :], y[:, q * D:(q + 1) * D]).then_inc(ln_step, 1)
                    if at_least(c, 2, M2):
                        dve.wait_ge(rstd_step, n * 2 - 2)
                    for q in range(TILES):
                        dve.wait_ge(ln_step, n * LN + 2 + q)
                        hold(dve, dve_passed)
                        nc.vector.bn_aggr(m[:, q, :], st[:, q, :]).then_inc(ln_step, 1)

            run_slots(dve, node_slot, 0, n_out + 1, M2, full // M2 * M2, M2)

        @block.tensor
        def _(pe):
            pe.wait_ge(consts_in, 16 * CONSTS)
            nc.tensor.matmul(ps[:, M_BANK, 0:D], wm_a[:, 0:P], wu2_a, start=True, stop=False)
            nc.tensor.matmul(ps[:, M_BANK, 0:D], wm_b[:, 0:P], wu2_b, start=False, stop=True)
            nc.tensor.matmul(ps[0:97, M_BANK + 1, 0:D], wm_a[:, P:225], wu2_a, start=True, stop=False)
            nc.tensor.matmul(ps[0:97, M_BANK + 1, 0:D], wm_b[:, P:225], wu2_b, start=False,
                             stop=True).then_inc(wc_ready, 1)
            pe.wait_ge(wc_copied, 2)
            pe.wait_ge(setup_done, DVE_SETUP)
            pe.wait_ge(scaled, 4)

            def bank_free(g, k):
                pe.wait_ge(t_free, number(g) * USES + k + 1)

            def transpose_x(g, k):
                pe.wait_ge(x_spread, number(g) * 4 + k + 1)
                bank_free(g, k + 1)
                for q in range(TILES):
                    last = nc.tensor.transpose(ps[:, T_BANK + (g[1] * USES + k + 1) % 2, q * P:(q + 1) * P],
                                               spread[:, q, k, :], ident_sb[:, :])
                last.then_inc(t_ready, 1)

            def transpose_e(g):
                pe.wait_ge(e_rests, number(g) * 2 + 2)
                bank_free(g, 0)
                bank = ps[:, T_BANK + g[1] * USES % 2, :].bitcast(BF16)
                for q in range(TILES):
                    last = nc.tensor.transpose(bank[0:3 * DE, q * P:(q + 1) * P],
                                               e3[g[1] % 2][:, q, :, :].rearrange("p k c -> p (k c)"), ident_bf[:, :])
                last.then_inc(t_ready, 1)

            def times_w3(g, h):
                bank_free(g, 5 + h)
                nc.tensor.matmul(ps[:, T_BANK + (g[1] * USES + 5 + h) % 2, :], w3_sb[64 * h:64 * h + 64, :],
                                 XY[g[1] % 2][64 * h:64 * h + 64, 0, :], start=True, stop=True).then_inc(t_ready, 1)

            def replicate(g, q):
                if q == 0:
                    pe.wait_ge(t_free, number(g) * USES + 3)
                pe.wait_ge(multiplied, number(g) * NQ + q + 1)
                nc.tensor.matmul(ps[:, E_BANK + q % 2, :], select_sb[:, q * P:(q + 1) * P], eT[g[1] % 2][:, :],
                                 start=True, stop=True).then_inc(e_ready, 1)

            def contract(g, n):
                if n == 0:
                    pe.wait_ge(multiplied, number(g) * NQ + NQ + 2)
                    if at_least(g, 1):
                        pe.wait_ge(V_copied, number(g))
                        pe.wait_ge(S_copied, number(g))
                if n == 4:
                    pe.wait_ge(parts_added_dve, number(g) * 2 + 2)
                    pe.wait_ge(parts_added_pool, number(g) * 2 + 2)

                def scalars(quarter, k, half, start, stop):
                    tile, w = (k, w1_sb[:, k, :]) if k < 4 else (10 + 6 * (k - 4), w2_sb[:, k - 4, :])
                    return nc.tensor.matmul(ps[32 * quarter:32 * quarter + 32, S_BANK, :], w[:, 32 * half:32 * half + 32],
                                            prod[g[1] % 2][:, tile, :], start=start, stop=stop)

                for i in range(3):
                    if n >= 4:
                        scalars(i, 3 * (n - 4) + i, 1, n == 4, n == 5)
                        continue
                    tile, w = (4 + 3 * n + i, w4_sb[:, n, :]) if n < 2 else (11 + 2 * (3 * (n - 2) + i), sum_sb[:, :])
                    vectors = nc.tensor.matmul(ps[32 * i:32 * i + 32, V_BANK, :], w, prod[g[1] % 2][:, tile, :],
                                               start=n == 0, stop=n == 3)
                if n == 3:
                    vectors.then_inc(V_ready, 1)
                last = scalars(3, n, 0, n == 0, n == 5)
                if n == 5:
                    last.then_inc(S_ready, 1)

            def messages(g, first):
                pe.wait_ge(S_copied, number(g) + 1)
                pe.wait_ge(V_copied, number(g) + 1)
                if at_least(g, 1):
                    pe.wait_ge(summed_copied, number(g))
                for q in (first, first + 1):
                    to = msg_ps[:, q // 2, q % 2 * D:(q % 2 + 1) * D]
                    nc.tensor.matmul(to, S_sb[g[1] % 2][:, q * P:(q + 1) * P], wc_s[:, :], start=True, stop=False)
                    last = nc.tensor.matmul(to, V_sb[g[1] % 2][:, q * P:(q + 1) * P], wc_v[:, :], start=False, stop=True)
                if first:
                    last.then_inc(msg_ready, 1)

            def sum_same(g):
                pe.wait_ge(msg_copied, number(g) + 1)
                pe.wait_ge(same_done, number(g) + 1)
                pe.wait_ge(same_low_done, number(g) + 1)
                for q in range(TILES):
                    nc.tensor.matmul(msg_ps[:, q // 2, q % 2 * D:(q % 2 + 1) * D], same[g[1] % 2][:, q, :],
                                     msg[g[1] % 2][:, q, :], start=True, stop=True)
                for q in range(TILES):
                    last = nc.tensor.matmul(sum_ps[:, q // 2, 2 * D + q % 2:2 * D + q % 2 + 1], same_low[g[1] % 2][:, q, :], ones_bf[:, :],
                                            start=True, stop=True)
                last.then_inc(summed_ready, 1)

            def slot(s):
                live = lambda d: not isinstance(s[0], int) or 0 <= number(s) + d < n_groups
                before, two_before, after = shift(s, -1), shift(s, -2), shift(s, 1)
                for q in range(NQ):
                    if live(0):
                        replicate(s, q)
                    if q == 0 and live(0):
                        transpose_x(s, 3)
                    if q < 2 and live(0):
                        times_w3(s, q)
                    if live(-2):
                        if q in (2, 4):
                            messages(two_before, q - 2)
                        if q == 6:
                            sum_same(two_before)
                    if live(1):
                        if q == 3:
                            transpose_e(after)
                        if q == 10:
                            transpose_x(after, 1)
                            transpose_x(after, 2)
                    if live(-1) and q in (4, 5, 7, 8, 9, 10):
                        contract(before, (4, 5, 7, 8, 9, 10).index(q))
                    if q == 7 and live(1):
                        transpose_x(after, 0)

            run_slots(pe, slot, -1, n_groups + 2, 8, (n_groups - 1) // M1 * M1)

            pe.wait_ge(summed_copied, n_groups)

            def node_slot(c):
                b = c[1] % 4
                pe.wait_ge(xT_in[c[1]], c[0] * 16 + 16)
                if at_least(c, 4, M2):
                    pe.wait_ge(ln_step, number(c, M2) * LN - 4 * LN + 1)
                for q in range(TILES):
                    to = ps[:, 2 * b + q // 2, q % 2 * D:(q % 2 + 1) * D]
                    nc.tensor.matmul(to, xT[c[1]][:, q * P:(q + 1) * P], wux_a[:, :], start=True, stop=False)
                    last = nc.tensor.matmul(to, xT[c[1]][:, TILES * P:TILES * D], wux_b[:, q, :],
                                            start=False, stop=True)
                last.then_inc(upd_ready, 1)

            run_slots(pe, node_slot, 0, n_out, M2, full // M2 * M2, M2)


def constants(n_nodes):
    import numpy as np

    r = np.arange(P)
    component = np.zeros((NQ, P), np.int64)
    for k in range(4):
        component[k] = 2 * k + r // 64
    for f in range(2):
        component[4 + f] = 4 * f + r // 32
        for i in range(3):
            component[6 + 3 * f + i] = 8 + 3 * (4 * f + r // 32) + i
    select = (np.arange(3 * DE)[:, None] % DE == component.reshape(1, -1)).astype(np.float32)
    sum_select = (r[:, None] % NV == np.arange(NV)[None, :]).astype(np.float32)
    lower = (r[:, None] < r[None, :]).astype(np.float32)
    trash = np.repeat((n_nodes + r)[:, None], TILES, 1).astype(np.float32)
    return {"ident": np.eye(P, dtype=np.float32), "select": select, "sum_select": sum_select,
            "lower": lower, "trash": trash}


def kernel(x, src, dst, edge_attr_32, node_vec1, L0_gnn_W1, L0_gnn_W2, L0_gnn_W3, L0_gnn_W4,
           L0_gnn_Wm, L0_gnn_bm, L0_gnn_Wu, L0_gnn_bu):
    import numpy as np
    import concourse.bacc as bacc
    from concourse.bass_utils import run_bass_kernel_spmd

    x, src, dst, e = (np.asarray(a) for a in (x, src, dst, edge_attr_32))
    W1, W2, W3, W4, Wm, bm, Wu, bu = (np.asarray(a) for a in (
        L0_gnn_W1, L0_gnn_W2, L0_gnn_W3, L0_gnn_W4, L0_gnn_Wm, L0_gnn_bm, L0_gnn_Wu, L0_gnn_bu))
    n_nodes, n_edges = x.shape[0], src.shape[0]
    groups = (n_edges + GE - 1) // GE
    pad = groups * GE - n_edges
    src_p = np.concatenate([src, np.full(pad, n_nodes, src.dtype)])
    dst_p = np.concatenate([dst, np.zeros(pad, dst.dtype)])
    e_p = np.concatenate([e, np.zeros((pad, DE), e.dtype)])
    vec = 64 + 3 * np.arange(NV)[None, :] + np.arange(3)[:, None]
    rows = np.concatenate([Wm[32:64]] * 3 + [Wm[0:32], Wm[vec.reshape(-1)], bm[None, :]])
    node_groups = (n_nodes + GE - 1) // GE
    x_p = np.concatenate([x, np.zeros((node_groups * GE - n_nodes, D), x.dtype)]
                         ).reshape(node_groups, P, TILES, D)
    arrays = {
        "x": x,
        "x_t": np.concatenate([
            x_p[..., :P].transpose(0, 3, 2, 1).reshape(node_groups, P, GE),
            x_p[..., P:].transpose(0, 2, 3, 1).reshape(node_groups, P, P)], axis=2),
        "dst_idx": dst_p.reshape(groups, P, TILES),
        "src_idx": src_p.reshape(groups, P, TILES),
        "src_row": src_p.reshape(groups, P, TILES).transpose(0, 2, 1).reshape(groups, 1, GE),
        "edge_attr": e_p.reshape(groups, P, TILES, DE),
        "w1": W1.transpose(1, 0, 2).reshape(4, P, NS).transpose(1, 0, 2),
        "w2": W2.transpose(1, 0, 2).reshape(2, P, NS).transpose(1, 0, 2),
        "w3": W3.reshape(64, 2, P).transpose(1, 0, 2).reshape(P, P),
        "w4": W4.transpose(1, 0, 2).reshape(2, P, NV).transpose(1, 0, 2),
        "wm_t": rows.T,
        "wu": Wu,
        "bu": bu.reshape(1, D),
        **constants(n_nodes),
    }
    nc = bacc.Bacc("TRN2", target_bir_lowering=False, num_devices=1)
    feeds, aps = {}, []
    for name, a in arrays.items():
        a = np.ascontiguousarray(a)
        feeds[f"in_{name}"] = a
        aps.append(nc.dram_tensor(f"in_{name}", a.shape, mybir.dt.from_np(a.dtype), kind="ExternalInput").ap())
    out = nc.dram_tensor("out", [n_nodes, D], F32, kind="ExternalOutput").ap()
    build(nc, *aps, out)
    result = run_bass_kernel_spmd(nc, [feeds], core_ids=[0])
    return result.results[0]["out"]
```
